# Optimizing a Trainium2 kernel written in Bass

```python
import numpy as np
import jax
import jax.numpy as jnp

def _softmax(x, axis=-1):
    return jax.nn.softmax(x, axis=axis)

def _gelu(x):
    return jax.nn.gelu(x, approximate=True)

def _silu(x):
    return jax.nn.silu(x)

def _sigmoid(x):
    return jax.nn.sigmoid(x)

def _layernorm(x, axis=-1, eps=1e-05):
    m = jnp.mean(x, axis=axis, keepdims=True)
    v = jnp.var(x, axis=axis, keepdims=True)
    return (x - m) / jnp.sqrt(v + eps)

def _scatter_add(tgt, idx, src, axis=0):
    return tgt.at[idx].add(src)

def _segment_sum(src, seg, n):
    return jax.ops.segment_sum(src, seg, n)
kernel_name = 'mk_adj_ffn_d1_adj_r2_51ba83'

def setup_inputs(seed: int=0):
    np.random.seed(seed)
    _w = jnp.asarray

    def _rec_inputs():
        import jax
        import jax.numpy as jnp
        _gk = jax.random.key(seed)
        x = -8.776e-05 + 1 * jax.random.normal(jax.random.fold_in(_gk, 1), (10000, 128), jnp.float32)
        _w = (1.0 + jnp.arange(10000, dtype=jnp.float32)) ** (-0.5)
        _w = _w / _w.mean()
        _pij = jnp.clip(0.0004 * _w[:, None] * _w[None, :], 0.0, 1.0)
        _a = jax.random.uniform(jax.random.fold_in(_gk, 2), (10000, 10000)) < _pij
        _a = jnp.logical_or(_a, jnp.eye(10000, dtype=bool))
        _af = _a.astype(jnp.float32)
        _af = _af * jax.random.uniform(jax.random.fold_in(_gk, 3), (10000, 10000), jnp.float32, 0.05, 1)
        adj = _af
        return (x, adj)
    x, adj = _rec_inputs()

    def _L0_gnn_setup():
        import jax, jax.numpy as jnp
        import numpy as np
        N_USER = 10000
        N_ITEM = 10000
        HID = 128
        key = jax.random.key(seed)
        k1, k2, k3, k4, k5, k6, k7 = jax.random.split(key, 7)
        scale = 1.0 / np.sqrt(HID)
        return {'user_feat': jax.random.normal(k1, (N_USER, HID), dtype=jnp.float32), 'item_feat': jax.random.normal(k2, (N_ITEM, HID), dtype=jnp.float32), 'adj': jax.random.uniform(k3, (N_USER, N_ITEM), dtype=jnp.float32), 'W_item': jax.random.uniform(k4, (HID, HID), dtype=jnp.float32, minval=-scale, maxval=scale), 'b_item': jax.random.uniform(k5, (HID,), dtype=jnp.float32, minval=-scale, maxval=scale), 'W_user': jax.random.uniform(k6, (HID, HID), dtype=jnp.float32, minval=-scale, maxval=scale), 'b_user': jax.random.uniform(k7, (HID,), dtype=jnp.float32, minval=-scale, maxval=scale)}
    _L0_gnn_all = _L0_gnn_setup()
    _L0_gnn_in = {k: v for k, v in _L0_gnn_all.items() if k in ('item_feat', 'W_item', 'b_item', 'W_user', 'b_user')}
    del _L0_gnn_all

    def _L0_ffn_setup():
        import jax, jax.numpy as jnp
        import numpy as np
        B, T, D, H, E = (16, 2048, 128, 256, 8)
        key = jax.random.key(seed)
        ks = jax.random.split(key, 5)
        x = jax.random.normal(ks[0], (B, T, D), dtype=jnp.float32)
        gate_w = jax.random.normal(ks[1], (D, E), dtype=jnp.float32) * 0.02
        gate_b = jnp.zeros((E,), dtype=jnp.float32)
        W1 = jax.random.normal(ks[2], (E, D, H), dtype=jnp.float32) * 0.02
        b1 = jnp.zeros((E, H), dtype=jnp.float32)
        W2 = jax.random.normal(ks[3], (E, H, D), dtype=jnp.float32) * 0.02
        b2 = jnp.zeros((E, D), dtype=jnp.float32)
        return {'x': x, 'gate_w': gate_w, 'gate_b': gate_b, 'W1': W1, 'b1': b1, 'W2': W2, 'b2': b2}
    _L0_ffn_all = _L0_ffn_setup()
    _L0_ffn_in = {k: v for k, v in _L0_ffn_all.items() if k in ('gate_w', 'gate_b', 'W1', 'b1', 'W2', 'b2')}
    del _L0_ffn_all
    return {'x': x, 'adj': adj, 'L0_gnn_item_feat': _L0_gnn_in['item_feat'], 'L0_gnn_W_item': _L0_gnn_in['W_item'], 'L0_gnn_b_item': _L0_gnn_in['b_item'], 'L0_gnn_W_user': _L0_gnn_in['W_user'], 'L0_gnn_b_user': _L0_gnn_in['b_user'], 'L0_ffn_gate_w': _L0_ffn_in['gate_w'], 'L0_ffn_gate_b': _L0_ffn_in['gate_b'], 'L0_ffn_W1': _L0_ffn_in['W1'], 'L0_ffn_b1': _L0_ffn_in['b1'], 'L0_ffn_W2': _L0_ffn_in['W2'], 'L0_ffn_b2': _L0_ffn_in['b2']}

def reference(x, adj, L0_gnn_item_feat, L0_gnn_W_item, L0_gnn_b_item, L0_gnn_W_user, L0_gnn_b_user, L0_ffn_gate_w, L0_ffn_gate_b, L0_ffn_W1, L0_ffn_b1, L0_ffn_W2, L0_ffn_b2):
    import jax
    import jax.numpy as jnp

    def _L0_gnn_ref(user_feat, item_feat, adj, W_item, b_item, W_user, b_user):
        import jax, jax.numpy as jnp
        import numpy as np
        N_USER = 10000
        N_ITEM = 10000
        HID = 128
        h = item_feat @ W_item.T + b_item
        b = user_feat @ W_user.T + b_user
        return jax.nn.relu(adj @ h + b)

    def _L0_ffn_ref(x, gate_w, gate_b, W1, b1, W2, b2):
        import jax, jax.numpy as jnp
        import numpy as np
        B, T, D, H, E = (16, 2048, 128, 256, 8)
        Bb, Tt, Dd = x.shape
        Ee = gate_w.shape[1]
        xf = x.reshape(-1, Dd)
        N = xf.shape[0]
        logits = xf @ gate_w + gate_b
        probs = jax.nn.softmax(logits, axis=-1)
        top2_vals, top2_idx = jax.lax.top_k(probs, 2)
        cw = jnp.zeros((N, Ee), dtype=xf.dtype).at[jnp.arange(N)[:, None], top2_idx].add(top2_vals)

        def step(acc, params):
            w1, bb1, w2, bb2, we = params
            h = jax.nn.gelu(xf @ w1 + bb1, approximate=False)
            y = h @ w2 + bb2
            return (acc + we[:, None] * y, None)
        out, _ = jax.lax.scan(step, jnp.zeros_like(xf), (W1, b1, W2, b2, cw.T))
        return out.reshape(Bb, Tt, Dd)
    x = x + _L0_gnn_ref(_layernorm(x, axis=-1), L0_gnn_item_feat, adj, L0_gnn_W_item, L0_gnn_b_item, L0_gnn_W_user, L0_gnn_b_user)
    x = x + _L0_ffn_ref(_layernorm(x, axis=-1)[None], L0_ffn_gate_w, L0_ffn_gate_b, L0_ffn_W1, L0_ffn_b1, L0_ffn_W2, L0_ffn_b2)[0]
    return x

_drawn_inputs = setup_inputs


def setup_inputs(seed=0):
    import zlib

    import numpy as np

    out = dict(_drawn_inputs(seed))
    spreads = {'L0_ffn_gate_b': (0.0, 0.578), 'L0_ffn_b1': (0.0, 0.8), 'L0_ffn_b2': (0.0, 0.435)}
    factors = {'L0_ffn_gate_w': 3.306, 'L0_ffn_W1': 7.752, 'L0_ffn_W2': 7.053}
    for name, (base, spread) in spreads.items():
        noise = np.random.default_rng([zlib.crc32(name.encode()), seed]).standard_normal(out[name].shape)
        drawn = base * np.exp(spread * noise) if base else spread * noise
        out[name] = jnp.asarray(drawn.astype(out[name].dtype))
    for name, factor in factors.items():
        out[name] = (out[name] * factor).astype(out[name].dtype)
    return out
```

```python
import concourse.bass as bass
from concourse import mybir
from contextlib import ExitStack

import numpy as np

P = 128
N = 10000
D = 128
E = 8
H = 256
HH = H // P
T = 500
NB = N // T
Q = 4
TQ = T // Q
KT = N // P
KREM = N - KT * P
CT = 2
NC = KT // CT
NPOS = NC + 1
RAW = 8
SPL = 4
GT = 3
NG = KT // GT
EPS = 1e-5
LO_ROW = 32
SEL_K = LO_ROW + E
GS = 10

assert NC * CT == KT and NG * GT == KT and NG % 2 == 0 and NPOS % RAW == 0 and NPOS % SPL == 0

T_CENTER, T_VAR, T_SCALE, T_GATE, T_TRANS, T_FFN, T_LAST = 1, 4, 8, 12, 17, 21, 38
U_CENTER, U_VAR, U_SCALE, U_DENSE = 13, 16, 20, 24
AHEAD = 2


def build(nc, adj_main, adj_rem, xT, itemT, item_rem, w_itemT, b_item_rows, w_userT, b_user, gate_w,
          gate_b_rows, w1, b1, w2, b2, center, mean, ident, before, pick, outT):
    fp32 = mybir.dt.float32
    fp32r = mybir.dt.float32r
    ALU = mybir.AluOpType
    ACT = mybir.ActivationFunctionType
    AX = mybir.AxisListType

    with ExitStack() as ctx:
        def sb(name, shape, dt=fp32):
            return ctx.enter_context(nc.sbuf_tensor(name, shape, dt))

        def bank(name):
            return ctx.enter_context(nc.psum_tensor(name, [P, 512], fp32))

        def sem(name):
            return ctx.enter_context(nc.semaphore(name))

        h_hi = sb("h_hi", [P, (KT + 1) * D], fp32r)
        h_lo = sb("h_lo", [P, (KT + 1) * D], fp32r)
        raw = [sb(f"raw{s}", [P, CT * T]) for s in range(RAW)]
        a_hi = [sb(f"a_hi{s}", [P, CT * T], fp32r) for s in range(SPL)]
        a_lo = [sb(f"a_lo{s}", [P, CT * T], fp32r) for s in range(SPL)]
        w_item_sb = sb("w_item_sb", [P, D])
        w_user_sb = sb("w_user_sb", [P, D])
        b_item_sb = sb("b_item_sb", [P, GT * D])
        b_user_sb = sb("b_user_sb", [P, 1])
        gate_w_sb = sb("gate_w_sb", [P, E])
        gate_b_sb = sb("gate_b_sb", [P, Q * E])
        w1_hi = sb("w1_hi", [P, E * H], fp32r)
        w1_lo = sb("w1_lo", [P, E * H], fp32r)
        b1_sb = sb("b1_sb", [P, E * HH])
        w2_sb = sb("w2_sb", [P, E * HH * D])
        b2_sb = sb("b2_sb", [E, D])
        center_sb = sb("center_sb", [P, P])
        mean_sb = sb("mean_sb", [P, 1])
        ident_sb = sb("ident_sb", [P, P])
        before_sb = sb("before_sb", [P, Q * E * E])
        pick_sb = sb("pick_sb", [SEL_K, E * P], fp32r)
        x_sb = sb("x_sb", [P, T])
        r_sb = sb("r_sb", [P, T])
        x1_sb = sb("x1_sb", [P, T])
        sq_sb = sb("sq_sb", [P, Q * P])
        var_sb = sb("var_sb", [TQ, Q])
        rstd_sb = sb("rstd_sb", [TQ, Q])
        power_sb = sb("power_sb", [TQ, Q])
        one_sb = sb("one_sb", [TQ, Q])
        xn_sb = sb("xn_sb", [P, T])
        o_sb = xn_sb
        xn_hi = sb("xn_hi", [P, T], fp32r)
        xn_lo = sb("xn_lo", [P, T], fp32r)
        logit_sb = sb("logit_sb", [TQ, Q * E])
        top_sb = sb("top_sb", [TQ, Q])
        shift_sb = sb("shift_sb", [TQ, Q * E])
        exp_sb = sb("exp_sb", [TQ, Q * E])
        sum_sb = sb("sum_sb", [TQ, Q])
        inv_sb = sb("inv_sb", [TQ, Q])
        prob_sb = sb("prob_sb", [TQ, Q * E])
        gt_sb = sb("gt_sb", [TQ, Q * E * E])
        eq_sb = sb("eq_sb", [TQ, Q * E * E])
        rank_sb = sb("rank_sb", [TQ, Q * E])
        cw_sb = sb("cw_sb", [TQ, Q * E])
        cwT_sb = sb("cwT_sb", [E, T])
        cw_parts = sb("cw_parts", [SEL_K, T], fp32r)
        g_sb = [sb(f"g_sb{j}", [P, T]) for j in range(HH)]
        gs_sb = [[sb(f"gs_sb{s}_{j}", [P, T]) for j in range(HH)] for s in range(2)]
        item_sb = [sq_sb, xn_sb]
        hf_sb = [r_sb, x1_sb]
        w1_raw = [g_sb[0], g_sb[1], gs_sb[0][0], gs_sb[0][1], x_sb]
        pick_raw = [gs_sb[1][0], gs_sb[1][1], logit_sb]

        acc = bank("acc")
        ps_x = bank("ps_x")
        ps_v = bank("ps_v")
        ps_g = bank("ps_g")
        ps_w = bank("ps_w")
        ps_z = [bank(f"ps_z{j}") for j in range(HH)]
        ps_y = bank("ps_y")
        ps_h = [ps_x, ps_v]

        const_landed = sem("const_landed")
        item_landed = [sem(f"item_landed{s}") for s in range(2)]
        h_product = sem("h_product")
        h_biased = sem("h_biased")
        h_hi_ready = sem("h_hi_ready")
        h_ready = sem("h_ready")
        item_rem_landed = sem("item_rem_landed")
        w1_hi_ready = sem("w1_hi_ready")
        w_ready = sem("w_ready")
        raw_landed = [sem(f"raw_landed{s}") for s in range(RAW)]
        hi_ready = sem("hi_ready")
        lo_ready = sem("lo_ready")
        adj_used = sem("adj_used")
        x_landed = sem("x_landed")
        u_centred = sem("u_centred")
        u_squared = sem("u_squared")
        u_kept = sem("u_kept")
        u_var = sem("u_var")
        u_var_eps = sem("u_var_eps")
        u_rstd = sem("u_rstd")
        u_copies = sem("u_copies")
        u_scale = sem("u_scale")
        u_norm = sem("u_norm")
        u_dense = sem("u_dense")
        relu_ready = sem("relu_ready")
        x1_ready = sem("x1_ready")
        t_centred = sem("t_centred")
        t_squared = sem("t_squared")
        t_kept = sem("t_kept")
        t_var = sem("t_var")
        t_var_eps = sem("t_var_eps")
        t_rstd = sem("t_rstd")
        t_copies = sem("t_copies")
        t_scale = sem("t_scale")
        power_ready = sem("power_ready")
        t_norm = sem("t_norm")
        t_norm_hi = sem("t_norm_hi")
        t_norm_lo = sem("t_norm_lo")
        logits_done = sem("logits_done")
        gate_step = sem("gate_step")
        shift_ready = sem("shift_ready")
        exp_ready = sem("exp_ready")
        cw_ready = sem("cw_ready")
        cwT_done = sem("cwT_done")
        cwT_ready = sem("cwT_ready")
        cw_hi_ready = sem("cw_hi_ready")
        parts_ready = sem("parts_ready")
        z_done = sem("z_done")
        spread_done = sem("spread_done")
        gelu_ready = sem("gelu_ready")
        gs_ready = sem("gs_ready")
        down_done = sem("down_done")
        y_done = sem("y_done")
        out_ready = sem("out_ready")
        stored = sem("stored")

        block = ctx.enter_context(nc.Block())

        def hi(ap):
            return ap.bitcast(fp32)

        consts = [(w_item_sb, w_itemT), (w_user_sb, w_userT), (b_item_sb, b_item_rows), (b_user_sb, b_user),
                  (gate_w_sb, gate_w), (gate_b_sb, gate_b_rows), (b1_sb, b1), (w2_sb, w2), (b2_sb, b2),
                  (center_sb, center), (mean_sb, mean), (ident_sb, ident), (before_sb, before)]
        staged = [(piece, w1, n * T, min(T, E * H - n * T)) for n, piece in enumerate(w1_raw)]
        staged_pick = [(piece, pick, n * T, min(T, E * P - n * T)) for n, piece in enumerate(pick_raw)]
        N_CONST = 16 * (len(consts) + len(staged) + len(staged_pick))

        @block.sync
        def _(sp):
            def load_step(i, p):
                s = p % RAW
                if isinstance(i, int) and i == 0 and p < RAW:
                    pass
                else:
                    sp.wait_ge(lo_ready, i * NPOS + (p - RAW + 1))
                if p < NC:
                    sp.dma_start(raw[s][:, :], adj_main[i, p]).then_inc(raw_landed[s], 16)
                else:
                    sp.dma_start(raw[s][0:KREM, 0:T], adj_rem[i]).then_inc(raw_landed[s], 16)

            def load_block(i, first):
                for p in range(NPOS):
                    load_step(i, p)
                    if p == RAW:
                        if not first:
                            sp.wait_ge(x1_ready, i)
                        else:
                            sp.wait_ge(w_ready, len(staged) + len(staged_pick))
                        sp.dma_start(x_sb[:, :], xT[i]).then_inc(x_landed, 16)

            load_block(0, True)
            with sp.Fori(1, NB) as i:
                load_block(i, False)

        @block.gpsimd
        def _(pool):
            for dst, src in consts[:3]:
                pool.dma_start(dst[:, :], src).then_inc(const_landed, 16)
            for s in range(2):
                pool.dma_start(item_sb[s][:, 0:GT * D], itemT[s]).then_inc(item_landed[s], 16)
            for dst, src in consts[3:]:
                pool.dma_start(dst[:, :], src).then_inc(const_landed, 16)
            for piece, src, at, width in staged + staged_pick:
                rows = src.shape[0]
                pool.dma_start(piece[0:rows, 0:width], src[:, at:at + width]).then_inc(const_landed, 16)
            with pool.Fori(1, NG // 2) as g2:
                for s in range(2):
                    pool.wait_ge(h_product, g2 * 2 + (s - 1))
                    pool.dma_start(item_sb[s][:, 0:GT * D], itemT[g2 * 2 + s]).then_inc(item_landed[s], 16)
            pool.wait_ge(h_product, NG - 1)
            pool.dma_start(item_sb[0][:, 0:KREM], item_rem).then_inc(item_rem_landed, 16)
            nc.gpsimd.memset(power_sb[:, :], -0.5).then_inc(power_ready, 1)
            nc.gpsimd.memset(one_sb[:, :], 1.0).then_inc(power_ready, 1)
            pool.wait_ge(power_ready, 2)

            def rstd(var_eps, rstd_done, copies, count):
                pool.wait_ge(var_eps, count)
                nc.gpsimd.tensor_tensor(rstd_sb[:, :], var_sb[:, :], power_sb[:, :], ALU.pow).then_inc(rstd_done, 1)
                pool.wait_ge(rstd_done, count)
                nc.gpsimd.tensor_tensor(sq_sb[0:TQ, :].rearrange("p (q c) -> p q c", c=P),
                                        rstd_sb[:, :].unsqueeze(2).to_broadcast([TQ, Q, P]),
                                        one_sb[:, :].unsqueeze(2).to_broadcast([TQ, Q, P]), ALU.mult).then_inc(copies, 1)

            rstd(u_var_eps, u_rstd, u_copies, 1)
            with pool.Fori(1, NB) as i:
                rstd(t_var_eps, t_rstd, t_copies, i)
                rstd(u_var_eps, u_rstd, u_copies, i + 1)
            rstd(t_var_eps, t_rstd, t_copies, NB)

        @block.scalar
        def _(act):
            with act.Fori(0, NG // 2) as g2:
                for s in range(2):
                    act.wait_ge(h_biased, g2 * 2 + (s + 1))
                    nc.scalar.activation(h_hi[:, bass.ds(g2 * (2 * GT * D) + s * GT * D, GT * D)], hf_sb[s][:, 0:GT * D],
                                         ACT.Copy).then_inc(h_hi_ready, 1)
            act.wait_ge(h_biased, NG + 1)
            nc.scalar.activation(h_hi[0:KREM, KT * D:(KT + 1) * D], hf_sb[0][0:KREM, 0:D],
                                 ACT.Copy).then_inc(h_hi_ready, 1)
            act.wait_ge(const_landed, N_CONST)
            for piece, _, at, width in staged:
                nc.scalar.activation(w1_hi[:, at:at + width], piece[:, 0:width], ACT.Copy).then_inc(w1_hi_ready, 1)

            def split_hi(i, p):
                s, q = p % RAW, p % SPL
                act.wait_ge(raw_landed[s], i * (16 * NPOS // RAW) + 16 * (p // RAW + 1))
                if not (isinstance(i, int) and i == 0 and p < SPL):
                    act.wait_ge(adj_used, i * NPOS + (p - SPL + 1))
                rows, cols = (P, CT * T) if p < NC else (KREM, T)
                nc.scalar.activation(a_hi[q][0:rows, 0:cols], raw[s][0:rows, 0:cols],
                                     ACT.Copy).then_inc(hi_ready, 1)

            def user(i, p):
                if p == U_CENTER + AHEAD + 1:
                    act.wait_ge(u_centred, i + 1)
                    nc.scalar.activation(sq_sb[:, 0:T], ps_x[:, 0:T], ACT.Square).then_inc(u_squared, 1)
                    nc.scalar.activation(xn_sb[:, :], ps_x[:, 0:T], ACT.Copy).then_inc(u_kept, 1)

            def tail(i, p):
                if p == 1:
                    act.wait_ge(adj_used, i * NPOS)
                    nc.scalar.activation(r_sb[:, :], acc[:, 0:T], ACT.Relu, bias=b_user_sb[:, 0:1]).then_inc(relu_ready, 1)
                if p == T_CENTER + AHEAD + 1:
                    act.wait_ge(t_centred, i)
                    nc.scalar.activation(sq_sb[:, 0:T], ps_x[:, 0:T], ACT.Square).then_inc(t_squared, 1)
                    if not (isinstance(i, int) and i == 1):
                        act.wait_ge(stored, i * 16 - 16)
                    nc.scalar.activation(xn_sb[:, :], ps_x[:, 0:T], ACT.Copy).then_inc(t_kept, 1)
                if p == T_GATE + AHEAD + 2:
                    act.wait_ge(shift_ready, i)
                    nc.scalar.activation(exp_sb[:, :], shift_sb[:, :], ACT.Exp).then_inc(exp_ready, 1)
                if p >= T_FFN + AHEAD and (p - T_FFN - AHEAD) % 2 == 0 and (p - T_FFN - AHEAD) // 2 < E:
                    e = (p - T_FFN - AHEAD) // 2
                    for j in range(HH):
                        act.wait_ge(z_done, i * (E * HH) + (HH * (e - E) + j + 1))
                        if j == 0:
                            if e > 0:
                                act.wait_ge(gs_ready, i * (E * HH) + HH * (e - E))
                        nc.scalar.activation(g_sb[j][:, :], ps_z[j][:, 0:T], ACT.Gelu,
                                             bias=b1_sb[:, e * HH + j:e * HH + j + 1]).then_inc(gelu_ready, 1)

            def store(i):
                act.wait_ge(out_ready, i)
                act.dma_start(outT[i - 1], o_sb[:, :]).then_inc(stored, 16)

            def one_pass(i, with_tail, with_store):
                for p in range(NPOS):
                    if with_store and p == 0:
                        store(i - 1)
                    split_hi(i, p)
                    if with_tail:
                        tail(i, p)
                    user(i, p)

            one_pass(0, False, False)
            one_pass(1, True, False)
            with act.Fori(2, NB) as i:
                one_pass(i, True, True)
            for p in range(NPOS):
                if p == 0:
                    store(NB - 1)
                tail(NB, p)
            store(NB)
            act.wait_ge(stored, 16 * NB)

        @block.vector
        def _(dve):
            nc.vector.memset(cw_parts[:, :].bitcast(fp32), 0.0).then_inc(gate_step, 1)
            dve.wait_ge(const_landed, N_CONST)

            for piece, _, at, width in staged_pick:
                nc.vector.tensor_copy(pick_sb[:, at:at + width], piece[0:SEL_K, 0:width]).then_inc(w_ready, 1)

            def h_bias(slot, rows, cols, product, free):
                dve.wait_ge(h_product, product)
                if free is not None:
                    dve.wait_ge(h_ready, free)
                nc.vector.tensor_tensor(hf_sb[slot][0:rows, 0:cols], ps_h[slot][0:rows, 0:cols],
                                        b_item_sb[0:rows, 0:cols], ALU.add).then_inc(h_biased, 1)

            def h_pair(g2):
                for s in range(2):
                    first = isinstance(g2, int)
                    h_bias(s, P, GT * D, g2 * 2 + (s + 1), None if first else g2 * 2 + (s - 1))
                for s in range(2):
                    at = g2 * (2 * GT * D) + s * GT * D
                    dve.wait_ge(h_hi_ready, g2 * 2 + (s + 1))
                    nc.vector.tensor_tensor(h_lo[:, bass.ds(at, GT * D)], hf_sb[s][:, 0:GT * D],
                                            hi(h_hi[:, bass.ds(at, GT * D)]), ALU.subtract).then_inc(h_ready, 1)

            h_pair(0)
            with dve.Fori(1, NG // 2) as g2:
                h_pair(g2)
            h_bias(0, KREM, D, NG + 1, NG)
            dve.wait_ge(h_hi_ready, NG + 1)
            nc.vector.tensor_tensor(h_lo[0:KREM, KT * D:(KT + 1) * D], hf_sb[0][0:KREM, 0:D],
                                    hi(h_hi[0:KREM, KT * D:(KT + 1) * D]), ALU.subtract).then_inc(h_ready, 1)
            for n, (piece, _, at, width) in enumerate(staged):
                dve.wait_ge(w1_hi_ready, n + 1)
                nc.vector.tensor_tensor(w1_lo[:, at:at + width], piece[:, 0:width], hi(w1_hi[:, at:at + width]),
                                        ALU.subtract).then_inc(w_ready, 1)

            def split_lo(i, p):
                s, q = p % RAW, p % SPL
                dve.wait_ge(hi_ready, i * NPOS + (p + 1))
                rows, cols = (P, CT * T) if p < NC else (KREM, T)
                nc.vector.tensor_tensor(a_lo[q][0:rows, 0:cols], raw[s][0:rows, 0:cols],
                                        hi(a_hi[q][0:rows, 0:cols]), ALU.subtract).then_inc(lo_ready, 1)

            def user(i, p):
                if p == U_VAR + AHEAD + 1:
                    dve.wait_ge(u_var, i + 1)
                    nc.vector.tensor_scalar(var_sb[:, :], ps_v[0:TQ, 0:Q], EPS, None, ALU.add).then_inc(u_var_eps, 1)
                if p == U_SCALE + AHEAD + 1:
                    dve.wait_ge(u_kept, i + 1)
                    dve.wait_ge(u_scale, i + 1)
                    nc.vector.tensor_tensor(xn_sb[:, :], ps_v[:, 0:T], xn_sb[:, :], ALU.mult).then_inc(u_norm, 1)

            def tail(i, p):
                if p == 2:
                    dve.wait_ge(relu_ready, i)
                    dve.wait_ge(x_landed, i * 16)
                    nc.vector.tensor_tensor(x1_sb[:, :], x_sb[:, :], r_sb[:, :], ALU.add).then_inc(x1_ready, 1)
                if p == T_VAR + AHEAD + 1:
                    dve.wait_ge(t_var, i)
                    nc.vector.tensor_scalar(var_sb[:, :], ps_v[0:TQ, 0:Q], EPS, None, ALU.add).then_inc(t_var_eps, 1)
                if p == T_SCALE + AHEAD + 1:
                    dve.wait_ge(t_kept, i)
                    dve.wait_ge(t_scale, i)
                    nc.vector.tensor_tensor(xn_sb[:, :], ps_v[:, 0:T], xn_sb[:, :], ALU.mult).then_inc(t_norm, 1)
                    dve.wait_ge(t_norm, i)
                    nc.vector.tensor_copy(xn_hi[:, :], xn_sb[:, :]).then_inc(t_norm_hi, 1)
                    dve.wait_ge(t_norm_hi, i)
                    nc.vector.tensor_tensor(xn_lo[:, :], xn_sb[:, :], hi(xn_hi[:, :]), ALU.subtract).then_inc(t_norm_lo, 1)
                if p == T_GATE + AHEAD + 1:
                    dve.wait_ge(logits_done, i)
                    nc.vector.tensor_tensor(logit_sb[:, :], ps_g[0:TQ, 0:Q * E], gate_b_sb[0:TQ, :], ALU.add).then_inc(gate_step, 1)
                    dve.wait_ge(gate_step, i * GS + (1 + 1 - GS))
                    by_e = logit_sb[:, :].rearrange("p (q e) -> p q e", e=E)
                    nc.vector.tensor_reduce(top_sb[:, :], by_e, AX.X, ALU.max).then_inc(gate_step, 1)
                    dve.wait_ge(gate_step, i * GS + (1 + 2 - GS))
                    nc.vector.tensor_tensor(shift_sb[:, :].rearrange("p (q e) -> p q e", e=E), by_e,
                                            top_sb[:, :].unsqueeze(2).to_broadcast([TQ, Q, E]),
                                            ALU.subtract).then_inc(shift_ready, 1)
                if p == T_GATE + AHEAD + 3:
                    dve.wait_ge(exp_ready, i)
                    exp_by_e = exp_sb[:, :].rearrange("p (q e) -> p q e", e=E)
                    nc.vector.tensor_reduce(sum_sb[:, :], exp_by_e, AX.X, ALU.add).then_inc(gate_step, 1)
                    dve.wait_ge(gate_step, i * GS + (1 + 3 - GS))
                    nc.vector.reciprocal(inv_sb[:, :], sum_sb[:, :]).then_inc(gate_step, 1)
                    dve.wait_ge(gate_step, i * GS + (1 + 4 - GS))
                    prob = prob_sb[:, :].rearrange("p (q e) -> p q e", e=E)
                    nc.vector.tensor_tensor(prob, exp_by_e, inv_sb[:, :].unsqueeze(2).to_broadcast([TQ, Q, E]),
                                            ALU.mult).then_inc(gate_step, 1)
                    dve.wait_ge(gate_step, i * GS + (1 + 5 - GS))
                    shape = [TQ, Q, E, E]
                    of_e = prob.unsqueeze(3).to_broadcast(shape)
                    of_f = prob.unsqueeze(2).to_broadcast(shape)
                    gt = gt_sb[:, :].rearrange("p (q e f) -> p q e f", e=E, f=E)
                    eq = eq_sb[:, :].rearrange("p (q e f) -> p q e f", e=E, f=E)
                    nc.vector.tensor_tensor(gt, of_f, of_e, ALU.is_gt).then_inc(gate_step, 1)
                    nc.vector.tensor_tensor(eq, of_f, of_e, ALU.is_equal).then_inc(gate_step, 1)
                    dve.wait_ge(gate_step, i * GS + (1 + 7 - GS))
                    nc.vector.tensor_tensor(eq_sb[:, :], eq_sb[:, :], before_sb[0:TQ, :], ALU.mult).then_inc(gate_step, 1)
                    dve.wait_ge(gate_step, i * GS + (1 + 8 - GS))
                    nc.vector.tensor_tensor(gt_sb[:, :], gt_sb[:, :], eq_sb[:, :], ALU.add).then_inc(gate_step, 1)
                    dve.wait_ge(gate_step, i * GS + (1 + 9 - GS))
                    nc.vector.tensor_reduce(rank_sb[:, :], gt_sb[:, :].rearrange("p (c f) -> p c f", f=E),
                                            AX.X, ALU.add).then_inc(gate_step, 1)
                    dve.wait_ge(gate_step, i * GS + (1 + 10 - GS))
                    nc.vector.scalar_tensor_tensor(out=cw_sb[:, :], in0=rank_sb[:, :], scalar=1.5, in1=prob_sb[:, :],
                                                   op0=ALU.is_lt, op1=ALU.mult).then_inc(cw_ready, 1)
                if p == T_TRANS + AHEAD + 1:
                    dve.wait_ge(cwT_done, i)
                    nc.vector.tensor_copy(cwT_sb[:, :], ps_g[0:E, 0:T]).then_inc(cwT_ready, 1)
                    dve.wait_ge(cwT_ready, i)
                    nc.vector.tensor_copy(cw_parts[0:E, :], cwT_sb[:, :]).then_inc(cw_hi_ready, 1)
                    dve.wait_ge(cw_hi_ready, i)
                    nc.vector.tensor_tensor(cw_parts[LO_ROW:LO_ROW + E, :], cwT_sb[:, :], hi(cw_parts[0:E, :]),
                                            ALU.subtract).then_inc(parts_ready, 1)
                if p >= T_FFN + AHEAD + 1 and (p - T_FFN - AHEAD - 1) % 2 == 0 and (p - T_FFN - AHEAD - 1) // 2 < E:
                    e = (p - T_FFN - AHEAD - 1) // 2
                    dve.wait_ge(spread_done, i * E + (e + 1 - E))
                    if e >= 2:
                        dve.wait_ge(down_done, i * E + (e - 1 - E))
                    for j in range(HH):
                        dve.wait_ge(gelu_ready, i * (E * HH) + (HH * (e - E) + j + 1))
                        nc.vector.tensor_tensor(gs_sb[e % 2][j][:, :], ps_w[:, 0:T], g_sb[j][:, :],
                                                ALU.mult).then_inc(gs_ready, 1)
                if p == NPOS - 1:
                    dve.wait_ge(y_done, i)
                    if not (isinstance(i, int) and i == 1):
                        dve.wait_ge(stored, i * 16 - 16)
                    nc.vector.tensor_tensor(o_sb[:, :], ps_y[:, 0:T], x1_sb[:, :], ALU.add).then_inc(out_ready, 1)

            def one_pass(i, with_tail):
                for p in range(NPOS):
                    split_lo(i, p)
                    if with_tail:
                        tail(i, p)
                    user(i, p)

            one_pass(0, False)
            one_pass(1, True)
            with dve.Fori(2, NB) as i:
                one_pass(i, True)
            for p in range(NPOS):
                tail(NB, p)

        @block.tensor
        def _(pe):
            def h_tile(slot, k, cols):
                return nc.tensor.matmul(ps_h[slot][0:cols, k * D:(k + 1) * D], item_sb[slot][:, k * P:k * P + cols],
                                        w_item_sb[:, :], start=True, stop=True)

            pe.wait_ge(const_landed, N_CONST)

            def variance(squared, var, count):
                pe.wait_ge(squared, count)
                for q in range(Q):
                    last = nc.tensor.matmul(ps_v[0:TQ, q:q + 1], sq_sb[:, q * TQ:(q + 1) * TQ], mean_sb[:, :],
                                            start=True, stop=True)
                last.then_inc(var, 1)

            def spread_scale(copies, scale, count):
                pe.wait_ge(copies, count)
                for q in range(Q):
                    last = nc.tensor.matmul(ps_v[:, q * TQ:(q + 1) * TQ], sq_sb[0:TQ, q * P:(q + 1) * P],
                                            ident_sb[0:TQ, 0:TQ], start=True, stop=True)
                last.then_inc(scale, 1)

            def h_group(g, s, g2, free):
                pe.wait_ge(item_landed[s], g2 * 16 + 16)
                if free is not None:
                    pe.wait_ge(h_biased, free)
                for k in range(GT):
                    last = h_tile(s, k, P)
                last.then_inc(h_product, 1)

            for s in range(2):
                h_group(s, s, 0, None)
            with pe.Fori(1, NG // 2) as g2:
                for s in range(2):
                    h_group(None, s, g2, g2 * 2 + (s - 1))
            pe.wait_ge(item_rem_landed, 16)
            pe.wait_ge(h_biased, NG)
            h_tile(0, 0, KREM).then_inc(h_product, 1)
            pe.wait_ge(h_ready, NG + 1)
            pe.wait_ge(w_ready, len(staged) + len(staged_pick))

            def adj_step(i, p):
                q = p % SPL
                pe.wait_ge(lo_ready, i * NPOS + (p + 1))
                tiles = CT if p < NC else 1
                rows = P if p < NC else KREM
                for c in range(tiles):
                    k = p * CT + c
                    w_hi = h_hi[0:rows, k * D:(k + 1) * D]
                    w_lo = h_lo[0:rows, k * D:(k + 1) * D]
                    m_hi = a_hi[q][0:rows, c * T:(c + 1) * T]
                    m_lo = a_lo[q][0:rows, c * T:(c + 1) * T]
                    nc.tensor.matmul(acc[:, 0:T], w_hi, m_hi, start=(k == 0), stop=False)
                    nc.tensor.matmul(acc[:, 0:T], w_hi, m_lo, start=False, stop=False)
                    last = nc.tensor.matmul(acc[:, 0:T], w_lo, m_hi, start=False, stop=(k == KT))
                last.then_inc(adj_used, 1)

            def user(i, p):
                if p == U_CENTER:
                    pe.wait_ge(x_landed, i * 16 + 16)
                    nc.tensor.matmul(ps_x[:, 0:T], center_sb[:, :], x_sb[:, :], start=True, stop=True).then_inc(u_centred, 1)
                if p == U_VAR:
                    variance(u_squared, u_var, i + 1)
                if p == U_SCALE:
                    spread_scale(u_copies, u_scale, i + 1)
                if p == U_DENSE:
                    pe.wait_ge(u_norm, i + 1)
                    nc.tensor.matmul(acc[:, 0:T], w_user_sb[:, :], xn_sb[:, :], start=False, stop=False).then_inc(u_dense, 1)

            def down(i, e):
                for j in range(HH):
                    pe.wait_ge(gs_ready, i * (E * HH) + (HH * (e - E) + j + 1))
                    last = nc.tensor.matmul(ps_y[:, 0:T], w2_sb[:, (e * HH + j) * D:(e * HH + j + 1) * D],
                                            gs_sb[e % 2][j][:, :], start=(e == 0 and j == 0), stop=False)
                last.then_inc(down_done, 1)

            def tail(i, p):
                if p == T_CENTER:
                    pe.wait_ge(x1_ready, i)
                    nc.tensor.matmul(ps_x[:, 0:T], center_sb[:, :], x1_sb[:, :], start=True, stop=True).then_inc(t_centred, 1)
                if p == T_VAR:
                    variance(t_squared, t_var, i)
                if p == T_SCALE:
                    spread_scale(t_copies, t_scale, i)
                if p == T_GATE:
                    pe.wait_ge(t_norm_lo, i)
                    for q in range(Q):
                        last = nc.tensor.matmul(ps_g[0:TQ, q * E:(q + 1) * E], xn_sb[:, q * TQ:(q + 1) * TQ],
                                                gate_w_sb[:, :], start=True, stop=True)
                    last.then_inc(logits_done, 1)
                if p == T_TRANS:
                    pe.wait_ge(cw_ready, i)
                    for q in range(Q):
                        last = nc.tensor.transpose(ps_g[0:E, q * TQ:(q + 1) * TQ], cw_sb[:, q * E:(q + 1) * E],
                                                   ident_sb[0:TQ, 0:TQ])
                    last.then_inc(cwT_done, 1)
                if p >= T_FFN and (p - T_FFN) % 2 == 0 and (p - T_FFN) // 2 < E:
                    e = (p - T_FFN) // 2
                    if e == 0:
                        pe.wait_ge(parts_ready, i)
                    else:
                        pe.wait_ge(gelu_ready, i * (E * HH) + HH * (e - E))
                    for j in range(HH):
                        at = e * H + j * P
                        nc.tensor.matmul(ps_z[j][:, 0:T], w1_hi[:, at:at + P], xn_hi[:, :], start=True, stop=False)
                        nc.tensor.matmul(ps_z[j][:, 0:T], w1_hi[:, at:at + P], xn_lo[:, :], start=False, stop=False)
                        nc.tensor.matmul(ps_z[j][:, 0:T], w1_lo[:, at:at + P], xn_hi[:, :], start=False,
                                         stop=True).then_inc(z_done, 1)
                    if e > 0:
                        down(i, e - 1)
                    nc.tensor.matmul(ps_w[:, 0:T], pick_sb[:, e * P:(e + 1) * P], cw_parts[:, :], start=True,
                                     stop=True).then_inc(spread_done, 1)
                if p == T_LAST:
                    down(i, E - 1)
                    nc.tensor.matmul(ps_y[:, 0:T], b2_sb[:, :], cwT_sb[:, :], start=False, stop=True).then_inc(y_done, 1)

            def one_pass(i, with_tail):
                for p in range(NPOS):
                    if p == 0 and with_tail:
                        pe.wait_ge(relu_ready, i)
                    adj_step(i, p)
                    if with_tail:
                        tail(i, p)
                    user(i, p)

            one_pass(0, False)
            with pe.Fori(1, NB) as i:
                one_pass(i, True)
            for p in range(NPOS):
                tail(NB, p)


def kernel(x, adj, L0_gnn_item_feat, L0_gnn_W_item, L0_gnn_b_item, L0_gnn_W_user, L0_gnn_b_user, L0_ffn_gate_w,
           L0_ffn_gate_b, L0_ffn_W1, L0_ffn_b1, L0_ffn_W2, L0_ffn_b2):
    import numpy as _np
    import concourse.bacc as _bacc
    from concourse import mybir as _mybir
    from concourse.bass_utils import run_bass_kernel_spmd as _run

    x, adj, item, w_item, b_item, w_user, b_user, gate_w, gate_b, w1, b1, w2, b2 = (
        _np.asarray(a) for a in (x, adj, L0_gnn_item_feat, L0_gnn_W_item, L0_gnn_b_item, L0_gnn_W_user, L0_gnn_b_user,
                                 L0_ffn_gate_w, L0_ffn_gate_b, L0_ffn_W1, L0_ffn_b1, L0_ffn_W2, L0_ffn_b2))
    eye = _np.eye(P, dtype=_np.float32)
    mean = _np.full((P, P), 1.0 / D, _np.float32)
    before = _np.tril(_np.ones((E, E), _np.float32), -1)
    pick = _np.zeros((SEL_K, E, P), _np.float32)
    for e in range(E):
        pick[e, e] = pick[LO_ROW + e, e] = 1.0
    blocks = adj.reshape(NB, T, N)
    arrays = {
        "adj_main": blocks[:, :, :KT * P].reshape(NB, T, NC, CT, P).transpose(0, 2, 4, 3, 1).reshape(NB, NC, P, CT * T),
        "adj_rem": blocks[:, :, KT * P:].transpose(0, 2, 1),
        "xT": x.reshape(NB, T, D).transpose(0, 2, 1),
        "itemT": item[:KT * P].reshape(NG, GT * P, D).transpose(0, 2, 1),
        "item_rem": item[KT * P:].T,
        "w_itemT": w_item.T,
        "b_item_rows": _np.broadcast_to(_np.tile(b_item, GT), (P, GT * D)),
        "w_userT": w_user.T,
        "b_user": b_user.reshape(D, 1),
        "gate_w": gate_w,
        "gate_b_rows": _np.broadcast_to(_np.tile(gate_b, Q), (P, Q * E)),
        "w1": w1.transpose(1, 0, 2).reshape(D, E * H),
        "b1": b1.reshape(E * HH, P).T,
        "w2": w2.reshape(E * HH, P, D).transpose(1, 0, 2).reshape(P, E * HH * D),
        "b2": b2,
        "center": eye - mean,
        "mean": mean[:, 0:1],
        "ident": eye,
        "before": _np.broadcast_to(_np.tile(before.reshape(-1), Q), (P, Q * E * E)),
        "pick": pick.reshape(SEL_K, E * P),
    }
    arrays = {f"in_{name}": _np.ascontiguousarray(a) for name, a in arrays.items()}
    nc = _bacc.Bacc("TRN2", target_bir_lowering=False, num_devices=1)
    args = [nc.dram_tensor(name, a.shape, _mybir.dt.from_np(a.dtype), kind="ExternalInput").ap()
            for name, a in arrays.items()]
    args.append(nc.dram_tensor("out", (NB, D, T), _mybir.dt.float32, kind="ExternalOutput").ap())
    build(nc, *args)
    r = _run(nc, [arrays], core_ids=[0])
    return r.results[0]["out"].transpose(0, 2, 1).reshape(N, D)
```

```python
import concourse.bass as bass
from concourse import mybir
from contextlib import ExitStack

import numpy as np

P = 128
N = 10000
D = 128
E = 8
H = 256
HH = H // P
T = 500
NB = N // T
Q = 4
TQ = T // Q
KT = N // P
KREM = N - KT * P
CT = 2
NC = KT // CT
NPOS = NC + 1
RAW = 8
SPL = 4
GT = 3
GD = GT * D
NG = KT // GT
NPAIR = NG // 2
ISLOTS = 4
I0 = RAW - ISLOTS
EPS = 1e-5
LO_ROW = 32
SEL_K = LO_ROW + E
GS = 9

assert NC * CT == KT and NG * GT == KT and NPAIR * 2 == NG and NPAIR % ISLOTS == 1
assert NPOS % RAW == 0 and NPOS % SPL == 0

T_TURN, T_BACK, T_GATE, T_TRANS = 2, 9, 12, 23
U_TURN, U_DENSE = 34, 38
STARTS = (27, 31, 35, 39, 44, 49, 54, 59, 64)
AHEAD = 2
A_RELU, A_TOKEN, A_NORM, A_EXP, A_SPLIT, A_SPREAD, A_STORE, A_KEEP, A_USER, A_FFN = 1, 5, 11, 16, 24, 26, 29, 36, 37, 4
V_X1, V_STATS, V_NORM, V_LO, V_FINISH, V_USTATS, V_UNORM, V_FFN = 2, 6, 8, 25, 28, 11, 33, 4
V_LOGITS, V_PROB, V_COMPARE, V_RANK, V_WEIGHT, V_SPREAD = 15, 17, 20, 21, 22, 26



def build(nc, adj_main, adj_rem, xT, xR, itemT, item_rem, w_itemT, b_item, w_userT, b_user, gate_w,
          gate_b_rows, w1, b1, w2, b2, ident, before, pick, outT):
    fp32 = mybir.dt.float32
    fp32r = mybir.dt.float32r
    ALU = mybir.AluOpType
    ACT = mybir.ActivationFunctionType
    AX = mybir.AxisListType

    with ExitStack() as ctx:
        def sb(name, shape, dt=fp32):
            return ctx.enter_context(nc.sbuf_tensor(name, shape, dt))

        def bank(name):
            return ctx.enter_context(nc.psum_tensor(name, [P, 512], fp32))

        def sem(name):
            return ctx.enter_context(nc.semaphore(name))

        h_hi = sb("h_hi", [P, (KT + 1) * D], fp32r)
        h_lo = sb("h_lo", [P, (KT + 1) * D], fp32r)
        raw = [sb(f"raw{s}", [P, CT * T]) for s in range(RAW)]
        a_hi = [sb(f"a_hi{s}", [P, CT * T], fp32r) for s in range(SPL)]
        a_lo = [sb(f"a_lo{s}", [P, CT * T], fp32r) for s in range(SPL)]
        w_item_sb = sb("w_item_sb", [P, D])
        w_user_sb = sb("w_user_sb", [P, D])
        b_user_sb = sb("b_user_sb", [P, 1])
        gate_w_sb = sb("gate_w_sb", [P, E])
        gate_b_sb = sb("gate_b_sb", [P, Q * E])
        w1_hi = sb("w1_hi", [P, E * H], fp32r)
        w1_lo = sb("w1_lo", [P, E * H], fp32r)
        b1_sb = sb("b1_sb", [P, E * HH])
        w2_sb = sb("w2_sb", [P, E * HH * D])
        b2_hi = sb("b2_hi", [SEL_K, D], fp32r)
        b2_lo = sb("b2_lo", [SEL_K, D], fp32r)
        ident_sb = sb("ident_sb", [P, P])
        before_sb = sb("before_sb", [P, Q * E * E])
        pick_sb = sb("pick_sb", [SEL_K, E * P], fp32r)
        power_sb = sb("power_sb", [TQ, Q])
        x_sb = sb("x_sb", [P, T])
        r_sb = sb("r_sb", [P, T])
        x1_sb = sb("x1_sb", [P, T])
        x1_kept = sb("x1_kept", [P, T])
        xn_sb = sb("xn_sb", [P, T])
        xn_hi = sb("xn_hi", [P, T], fp32r)
        xn_lo = sb("xn_lo", [P, T], fp32r)
        xr_sb = sb("xr_sb", [P, Q * D])
        xt_sb = sb("xt_sb", [P, Q * D])
        stats_sb = [sb(f"stats_sb{n}", [TQ, Q * 6]) for n in range(2)]
        mv_sb = [sb(f"mv_sb{n}", [TQ, Q * 2]) for n in range(2)]
        var_sb = [sb(f"var_sb{n}", [TQ, Q]) for n in range(2)]
        rstd_sb = [sb(f"rstd_sb{n}", [TQ, Q]) for n in range(2)]
        logit_sb = sb("logit_sb", [TQ, Q * E])
        top_sb = sb("top_sb", [TQ, Q])
        shift_sb = sb("shift_sb", [TQ, Q * E])
        exp_sb = sb("exp_sb", [TQ, Q * E])
        sum_sb = sb("sum_sb", [TQ, Q])
        inv_sb = sb("inv_sb", [TQ, Q])
        prob_sb = sb("prob_sb", [TQ, Q * E])
        rank_sb = sb("rank_sb", [TQ, Q * E])
        cw_sb = sb("cw_sb", [TQ, Q * E])
        cw_parts = sb("cw_parts", [SEL_K, T], fp32r)
        g_sb = [sb(f"g_sb{j}", [P, T]) for j in range(HH)]
        gs_sb = [[sb(f"gs_sb{s}_{j}", [P, T]) for j in range(HH)] for s in range(2)]
        o_sb = r_sb
        gt_sb = xt_sb[0:TQ, 0:Q * E * E]
        eq_sb = xt_sb[0:TQ, Q * E * E:2 * Q * E * E]

        acc = bank("acc")
        ps_x = bank("ps_x")
        ps_v = bank("ps_v")
        ps_g = bank("ps_g")
        ps_w = bank("ps_w")
        ps_z = [bank(f"ps_z{j}") for j in range(HH)]
        ps_y = bank("ps_y")
        ps_h = [ps_x, ps_v, ps_g, ps_w]

        first_landed = sem("first_landed")
        const_landed = sem("const_landed")
        item_landed = [sem(f"item_landed{s}") for s in range(ISLOTS)]
        bias_hi_ready = sem("bias_hi_ready")
        bias_ready = sem("bias_ready")
        h_product = sem("h_product")
        h_hi_ready = sem("h_hi_ready")
        h_ready = sem("h_ready")
        w_hi_ready = sem("w_hi_ready")
        w_ready = sem("w_ready")
        power_ready = sem("power_ready")
        raw_landed = [sem(f"raw_landed{s}") for s in range(RAW)]
        hi_ready = sem("hi_ready")
        lo_ready = sem("lo_ready")
        adj_used = sem("adj_used")
        x_landed = sem("x_landed")
        xr_landed = sem("xr_landed")
        u_stats = sem("u_stats")
        u_moments = sem("u_moments")
        u_var = sem("u_var")
        u_rstd = sem("u_rstd")
        u_normed = sem("u_normed")
        u_turned = sem("u_turned")
        u_kept = sem("u_kept")
        u_dense = sem("u_dense")
        relu_ready = sem("relu_ready")
        x1_ready = sem("x1_ready")
        t_turned = sem("t_turned")
        xt_ready = sem("xt_ready")
        t_stats = sem("t_stats")
        t_moments = sem("t_moments")
        var_clear = sem("var_clear")
        t_var = sem("t_var")
        t_rstd = sem("t_rstd")
        t_normed = sem("t_normed")
        t_back = sem("t_back")
        xn_hi_ready = sem("xn_hi_ready")
        xn_ready = sem("xn_ready")
        xn_lo_ready = sem("xn_lo_ready")
        logits_done = sem("logits_done")
        gate_step = sem("gate_step")
        shift_ready = sem("shift_ready")
        exp_ready = sem("exp_ready")
        rank_ready = sem("rank_ready")
        cw_ready = sem("cw_ready")
        cwT_done = sem("cwT_done")
        cw_hi_ready = sem("cw_hi_ready")
        parts_ready = sem("parts_ready")
        z_done = sem("z_done")
        spread_done = sem("spread_done")
        gelu_ready = sem("gelu_ready")
        gs_ready = sem("gs_ready")
        down_done = sem("down_done")
        kept_ready = sem("kept_ready")
        out_ready = sem("out_ready")
        stored = sem("stored")

        block = ctx.enter_context(nc.Block())

        def val(ap):
            return ap.bitcast(fp32)

        def quarters(ap, width):
            return ap.rearrange("p (q c) -> p q c", c=width)

        b_item_raw = xn_sb
        b2_raw = xt_sb
        w1_raw = [(piece, n * T, min(T, E * H - n * T))
                  for n, piece in enumerate([g_sb[0], g_sb[1], gs_sb[0][0], gs_sb[0][1], gs_sb[1][0]])]
        pick_raw = [(piece, n * T, min(T, E * P - n * T)) for n, piece in enumerate([gs_sb[1][1], r_sb, x1_sb])]
        N_FIRST = 16 * (2 + len(pick_raw))
        consts = [(ident_sb, ident), (w_user_sb, w_userT), (b_user_sb, b_user), (gate_w_sb, gate_w),
                  (gate_b_sb, gate_b_rows), (b1_sb, b1), (w2_sb, w2), (before_sb, before)]
        N_CONST = 16 * (len(consts) + 1 + len(w1_raw))

        @block.sync
        def _(sp):
            def load_items(n, s):
                sp.dma_start(raw[I0 + s][:, 0:2 * GD], itemT[n]).then_inc(item_landed[s], 16)

            def load_step(i, p):
                s = p % RAW
                if isinstance(i, int) and i == 0 and p < RAW:
                    if s >= I0:
                        sp.wait_ge(h_product, NG + 1)
                else:
                    sp.wait_ge(lo_ready, i * NPOS + (p - RAW + 1))
                if p < NC:
                    sp.dma_start(raw[s][:, :], adj_main[i, p]).then_inc(raw_landed[s], 16)
                else:
                    sp.dma_start(raw[s][0:KREM, 0:T], adj_rem[i]).then_inc(raw_landed[s], 16)

            def load_xr(i):
                sp.dma_start(xr_sb[0:TQ, :], xR[i]).then_inc(xr_landed, 16)

            def load_x(i):
                sp.dma_start(x_sb[:, :], xT[i]).then_inc(x_landed, 16)

            for s in range(ISLOTS):
                load_items(s, s)
            with sp.Fori(1, NPAIR // ISLOTS) as r:
                for s in range(ISLOTS):
                    sp.wait_ge(h_product, r * (2 * ISLOTS) + (2 * s + 2 - 2 * ISLOTS))
                    load_items(r * ISLOTS + s, s)
            sp.wait_ge(h_product, NG - 2 * ISLOTS)
            load_items(NPAIR - 1, 0)
            sp.wait_ge(h_product, NG - 2 * ISLOTS + 2)
            sp.dma_start(raw[I0 + 1][:, 0:KREM], item_rem).then_inc(item_landed[1], 16)

            for p in range(NPOS):
                load_step(0, p)
                if p == I0 - 1:
                    load_xr(0)
                if p == RAW:
                    load_x(0)
            with sp.Fori(1, NB) as i:
                for p in range(NPOS):
                    load_step(i, p)
                    if p == 2:
                        sp.wait_ge(u_turned, i)
                        load_xr(i)
                    if p == RAW:
                        sp.wait_ge(x1_ready, i)
                        load_x(i)

        @block.gpsimd
        def _(pool):
            nc.gpsimd.memset(power_sb[:, :], -0.5).then_inc(power_ready, 1)
            for dst, src in consts:
                pool.dma_start(dst[:, :], src).then_inc(const_landed, 16)
            pool.dma_start(b2_raw[0:SEL_K, 0:D], b2).then_inc(const_landed, 16)
            for piece, at, width in w1_raw:
                pool.dma_start(piece[:, 0:width], w1[:, at:at + width]).then_inc(const_landed, 16)
            pool.wait_ge(power_ready, 1)

            def user(i):
                pool.wait_ge(u_var, i + 1)
                nc.gpsimd.tensor_tensor(rstd_sb[0][:, :], var_sb[0][:, :], power_sb[:, :], ALU.pow).then_inc(u_rstd, 1)

            def tail(i):
                pool.wait_ge(t_var, i)
                nc.gpsimd.tensor_tensor(rstd_sb[1][:, :], var_sb[1][:, :], power_sb[:, :], ALU.pow).then_inc(t_rstd, 1)

            user(0)
            with pool.Fori(1, NB) as i:
                tail(i)
                user(i)
            tail(NB)

        @block.scalar
        def _(act):
            act.dma_start(w_item_sb[:, :], w_itemT).then_inc(first_landed, 16)
            act.dma_start(b_item_raw[0:1, 0:D], b_item).then_inc(first_landed, 16)
            for piece, at, width in pick_raw:
                act.dma_start(piece[0:SEL_K, 0:width], pick[:, at:at + width]).then_inc(first_landed, 16)

            def h_hi_part(b, at, rows, cols, product):
                act.wait_ge(h_product, product)
                nc.scalar.activation(h_hi[0:rows, at], ps_h[b][0:rows, 0:cols], ACT.Copy).then_inc(h_hi_ready, 1)

            with act.Fori(0, NG // 4) as r:
                for b in range(4):
                    h_hi_part(b, bass.ds(r * (4 * GD) + b * GD, GD), P, GD, r * 4 + (b + 1))
            for b in range(NG % 4):
                g = NG // 4 * 4 + b
                h_hi_part(b, slice(g * GD, (g + 1) * GD), P, GD, g + 1)
            h_hi_part(NG % 4, slice(KT * D, (KT + 1) * D), KREM, D, NG + 1)

            def split_hi(i, p):
                s, q = p % RAW, p % SPL
                act.wait_ge(raw_landed[s], i * (16 * NPOS // RAW) + 16 * (p // RAW + 1))
                if not (isinstance(i, int) and i == 0 and p < SPL):
                    act.wait_ge(adj_used, i * NPOS + (p - SPL + 1))
                rows, cols = (P, CT * T) if p < NC else (KREM, T)
                nc.scalar.activation(a_hi[q][0:rows, 0:cols], raw[s][0:rows, 0:cols],
                                     ACT.Copy).then_inc(hi_ready, 1)

            def weights(p):
                n, odd = divmod(p - STARTS[0], 2)
                if p >= STARTS[0] and odd == 0 and n < len(w1_raw):
                    piece, at, width = w1_raw[n]
                    act.wait_ge(const_landed, N_CONST)
                    nc.scalar.activation(w1_hi[:, at:at + width], piece[:, 0:width], ACT.Copy).then_inc(w_hi_ready, 1)

            def user(i, p):
                if p == A_USER:
                    act.wait_ge(u_turned, i + 1)
                    nc.scalar.activation(xn_sb[:, :], ps_x[:, 0:T], ACT.Copy).then_inc(u_kept, 1)

            def tail(i, p):
                if p == A_RELU:
                    act.wait_ge(adj_used, i * NPOS)
                    nc.scalar.activation(r_sb[:, :], acc[:, 0:T], ACT.Relu, bias=b_user_sb[:, 0:1]).then_inc(relu_ready, 1)
                if p == A_TOKEN:
                    act.wait_ge(t_turned, i)
                    nc.scalar.activation(xt_sb[0:TQ, :], ps_v[0:TQ, :], ACT.Copy).then_inc(xt_ready, 1)
                if p == A_NORM:
                    act.wait_ge(t_back, i)
                    nc.scalar.activation(xn_sb[:, :], ps_x[:, 0:T], ACT.Copy).then_inc(xn_ready, 1)
                if p == A_SPLIT:
                    act.wait_ge(xn_ready, i)
                    if not (isinstance(i, int) and i == 1):
                        act.wait_ge(z_done, i * (E * HH) - E * HH)
                    nc.scalar.activation(xn_hi[:, :], xn_sb[:, :], ACT.Copy).then_inc(xn_hi_ready, 1)
                if p == A_EXP:
                    act.wait_ge(shift_ready, i)
                    nc.scalar.activation(exp_sb[:, :], shift_sb[:, :], ACT.Exp).then_inc(exp_ready, 1)
                if p == A_KEEP:
                    if not (isinstance(i, int) and i == 1):
                        act.wait_ge(out_ready, i - 1)
                        act.wait_ge(stored, i * 16 - 16)
                    act.wait_ge(x1_ready, i)
                    nc.scalar.activation(x1_kept[:, :], x1_sb[:, :], ACT.Copy).then_inc(kept_ready, 1)
                if p == A_SPREAD:
                    act.wait_ge(cwT_done, i)
                    nc.scalar.activation(cw_parts[0:E, :], ps_g[0:E, 0:T], ACT.Copy).then_inc(cw_hi_ready, 1)

            def experts(i, p):
                if p - A_FFN in STARTS[:E]:
                    e = STARTS.index(p - A_FFN)
                    if not (isinstance(i, int) and i == 1 and e == 0):
                        act.wait_ge(gs_ready, i * (E * HH) + HH * (e - E))
                    for j in range(HH):
                        act.wait_ge(z_done, i * (E * HH) + (HH * (e - E) + j + 1))
                        nc.scalar.activation(g_sb[j][:, :], ps_z[j][:, 0:T], ACT.Gelu,
                                             bias=b1_sb[:, e * HH + j:e * HH + j + 1]).then_inc(gelu_ready, 1)

            def finish(i):
                act.wait_ge(out_ready, i - 1)
                act.dma_start(outT[i - 2], o_sb[:, :]).then_inc(stored, 16)

            def one_pass(i, with_tail, with_finish):
                for p in range(NPOS):
                    split_hi(i, p)
                    if not with_tail:
                        weights(p)
                    if with_tail:
                        tail(i, p)
                    if with_finish:
                        experts(i - 1, p + NPOS)
                        if p == A_STORE:
                            finish(i)
                    if with_tail:
                        experts(i, p)
                    user(i, p)

            one_pass(0, False, False)
            one_pass(1, True, False)
            with act.Fori(2, NB) as i:
                one_pass(i, True, True)
            for p in range(NPOS):
                tail(NB, p)
                experts(NB - 1, p + NPOS)
                if p == A_STORE:
                    finish(NB)
                experts(NB, p)
            for p in range(NPOS, 2 * NPOS):
                experts(NB, p)
            finish(NB + 1)
            act.wait_ge(stored, 16 * NB)

        @block.vector
        def _(dve):
            nc.vector.memset(val(cw_parts[:, :]), 0.0).then_inc(bias_hi_ready, 1)
            dve.wait_ge(first_landed, N_FIRST)
            for piece, at, width in pick_raw:
                nc.vector.tensor_copy(pick_sb[:, at:at + width], piece[0:SEL_K, 0:width]).then_inc(bias_ready, 1)
            dve.wait_ge(bias_hi_ready, 1)
            bias = b_item_raw[0:1, 0:D].unsqueeze(1).to_broadcast([1, GT, D])
            row_hi = quarters(cw_parts[0:1, 0:GD], D)
            nc.vector.tensor_copy(row_hi, bias).then_inc(bias_hi_ready, 1)
            dve.wait_ge(bias_hi_ready, 2)
            nc.vector.tensor_tensor(quarters(cw_parts[LO_ROW:LO_ROW + 1, 0:GD], D), bias, val(row_hi),
                                    ALU.subtract).then_inc(bias_ready, 1)

            def h_lo_part(b, at, rows, cols, ready):
                dve.wait_ge(h_hi_ready, ready)
                nc.vector.tensor_tensor(h_lo[0:rows, at], ps_h[b][0:rows, 0:cols], val(h_hi[0:rows, at]),
                                        ALU.subtract).then_inc(h_ready, 1)

            with dve.Fori(0, NG // 4) as r:
                for b in range(4):
                    h_lo_part(b, bass.ds(r * (4 * GD) + b * GD, GD), P, GD, r * 4 + (b + 1))
            for b in range(NG % 4):
                g = NG // 4 * 4 + b
                h_lo_part(b, slice(g * GD, (g + 1) * GD), P, GD, g + 1)
            h_lo_part(NG % 4, slice(KT * D, (KT + 1) * D), KREM, D, NG + 1)

            def split_lo(i, p):
                s, q = p % RAW, p % SPL
                dve.wait_ge(hi_ready, i * NPOS + (p + 1))
                rows, cols = (P, CT * T) if p < NC else (KREM, T)
                nc.vector.tensor_tensor(a_lo[q][0:rows, 0:cols], raw[s][0:rows, 0:cols],
                                        val(a_hi[q][0:rows, 0:cols]), ALU.subtract).then_inc(lo_ready, 1)

            def weights(p):
                n, odd = divmod(p - STARTS[0], 2)
                if p >= STARTS[0] and odd == 1 and n < len(w1_raw):
                    piece, at, width = w1_raw[n]
                    dve.wait_ge(w_hi_ready, n + 1)
                    nc.vector.tensor_tensor(w1_lo[:, at:at + width], piece[:, 0:width], val(w1_hi[:, at:at + width]),
                                            ALU.subtract).then_inc(w_ready, 1)
                if p == STARTS[0]:
                    dve.wait_ge(const_landed, N_CONST)
                    nc.vector.tensor_copy(b2_hi[:, :], b2_raw[0:SEL_K, 0:D]).then_inc(w_ready, 1)
                    dve.wait_ge(w_ready, 1)
                    nc.vector.tensor_tensor(b2_lo[:, :], b2_raw[0:SEL_K, 0:D], val(b2_hi[:, :]),
                                            ALU.subtract).then_inc(w_ready, 1)

            def moments(n, rows, stats_done, moments_done, var_done, count):
                for q in range(Q):
                    last = nc.vector.bn_stats(stats_sb[n][:, q * 6:(q + 1) * 6], rows[:, q * D:(q + 1) * D])
                last.then_inc(stats_done, 1)
                dve.wait_ge(stats_done, count)
                nc.vector.memset(var_sb[n][:, :], 0.0).then_inc(var_clear, 1)
                for q in range(Q):
                    last = nc.vector.bn_aggr(mv_sb[n][:, q * 2:(q + 1) * 2], stats_sb[n][:, q * 6:(q + 1) * 6])
                last.then_inc(moments_done, 1)
                dve.wait_ge(moments_done, count)
                nc.vector.tensor_scalar(var_sb[n][:, :], quarters(mv_sb[n][:, :], 2)[:, :, 1], EPS, None,
                                        ALU.add).then_inc(var_done, 1)

            def normalise(n, out, rows, done):
                for q in range(Q):
                    last = nc.vector.tensor_scalar(out[:, q * D:(q + 1) * D], rows[:, q * D:(q + 1) * D],
                                                   mv_sb[n][:, 2 * q:2 * q + 1], rstd_sb[n][:, q:q + 1],
                                                   ALU.subtract, ALU.mult)
                last.then_inc(done, 1)

            def user(i, p):
                if p == V_USTATS:
                    dve.wait_ge(xr_landed, i * 16 + 16)
                    moments(0, xr_sb[0:TQ, :], u_stats, u_moments, u_var, i + 1)
                if p == V_UNORM:
                    dve.wait_ge(u_rstd, i + 1)
                    normalise(0, xr_sb[0:TQ, :], xr_sb[0:TQ, :], u_normed)

            def tail(i, p):
                if p == V_X1:
                    dve.wait_ge(relu_ready, i)
                    dve.wait_ge(x_landed, i * 16)
                    if not (isinstance(i, int) and i == 1):
                        dve.wait_ge(kept_ready, i - 1)
                    nc.vector.tensor_tensor(x1_sb[:, :], x_sb[:, :], r_sb[:, :], ALU.add).then_inc(x1_ready, 1)
                if p == V_STATS:
                    dve.wait_ge(xt_ready, i)
                    moments(1, xt_sb[0:TQ, :], t_stats, t_moments, t_var, i)
                if p == V_NORM:
                    dve.wait_ge(t_rstd, i)
                    normalise(1, xt_sb[0:TQ, :], xt_sb[0:TQ, :], t_normed)
                if p == V_LO:
                    dve.wait_ge(xn_hi_ready, i)
                    nc.vector.tensor_tensor(xn_lo[:, :], xn_sb[:, :], val(xn_hi[:, :]), ALU.subtract).then_inc(xn_lo_ready, 1)
                step = i * GS - GS
                by_e = quarters(logit_sb[:, :], E)
                exp_by_e = quarters(exp_sb[:, :], E)
                prob = quarters(prob_sb[:, :], E)
                if p == V_LOGITS:
                    dve.wait_ge(logits_done, i)
                    nc.vector.tensor_tensor(logit_sb[:, :], ps_g[0:TQ, 0:Q * E], gate_b_sb[0:TQ, :], ALU.add).then_inc(gate_step, 1)
                    dve.wait_ge(gate_step, step + 1)
                    nc.vector.tensor_reduce(top_sb[:, :], by_e, AX.X, ALU.max).then_inc(gate_step, 1)
                    dve.wait_ge(gate_step, step + 2)
                    nc.vector.tensor_tensor(quarters(shift_sb[:, :], E), by_e, top_sb[:, :].unsqueeze(2).to_broadcast([TQ, Q, E]),
                                            ALU.subtract).then_inc(shift_ready, 1)
                if p == V_PROB:
                    dve.wait_ge(exp_ready, i)
                    nc.vector.tensor_reduce(sum_sb[:, :], exp_by_e, AX.X, ALU.add).then_inc(gate_step, 1)
                    dve.wait_ge(gate_step, step + 3)
                    nc.vector.reciprocal(inv_sb[:, :], sum_sb[:, :]).then_inc(gate_step, 1)
                    dve.wait_ge(gate_step, step + 4)
                    nc.vector.tensor_tensor(prob, exp_by_e, inv_sb[:, :].unsqueeze(2).to_broadcast([TQ, Q, E]),
                                            ALU.mult).then_inc(gate_step, 1)
                if p == V_COMPARE:
                    shape = [TQ, Q, E, E]
                    of_e = prob.unsqueeze(3).to_broadcast(shape)
                    of_f = prob.unsqueeze(2).to_broadcast(shape)
                    dve.wait_ge(gate_step, step + 5)
                    nc.vector.tensor_tensor(gt_sb.rearrange("p (q e f) -> p q e f", e=E, f=E), of_f, of_e,
                                            ALU.is_gt).then_inc(gate_step, 1)
                    nc.vector.tensor_tensor(eq_sb.rearrange("p (q e f) -> p q e f", e=E, f=E), of_f, of_e,
                                            ALU.is_equal).then_inc(gate_step, 1)
                if p == V_RANK:
                    dve.wait_ge(gate_step, step + 7)
                    nc.vector.tensor_tensor(eq_sb, eq_sb, before_sb[0:TQ, :], ALU.mult).then_inc(gate_step, 1)
                    dve.wait_ge(gate_step, step + 8)
                    nc.vector.tensor_tensor(gt_sb, gt_sb, eq_sb, ALU.add).then_inc(gate_step, 1)
                if p == V_WEIGHT:
                    dve.wait_ge(gate_step, step + 9)
                    nc.vector.tensor_reduce(rank_sb[:, :], gt_sb.rearrange("p (c f) -> p c f", f=E),
                                            AX.X, ALU.add).then_inc(rank_ready, 1)
                    dve.wait_ge(rank_ready, i)
                    nc.vector.scalar_tensor_tensor(out=cw_sb[:, :], in0=rank_sb[:, :], scalar=1.5, in1=prob_sb[:, :],
                                                   op0=ALU.is_lt, op1=ALU.mult).then_inc(cw_ready, 1)
                if p == V_SPREAD:
                    dve.wait_ge(cw_hi_ready, i)
                    nc.vector.tensor_tensor(cw_parts[LO_ROW:LO_ROW + E, :], ps_g[0:E, 0:T], val(cw_parts[0:E, :]),
                                            ALU.subtract).then_inc(parts_ready, 1)

            def experts(i, p):
                if p - V_FFN in STARTS[:E]:
                    e = STARTS.index(p - V_FFN)
                    dve.wait_ge(spread_done, i * E + (e + 1 - E))
                    if e >= 2:
                        dve.wait_ge(down_done, i * E + (e - 1 - E))
                    for j in range(HH):
                        dve.wait_ge(gelu_ready, i * (E * HH) + (HH * (e - E) + j + 1))
                        nc.vector.tensor_tensor(gs_sb[e % 2][j][:, :], ps_w[:, 0:T], g_sb[j][:, :],
                                                ALU.mult).then_inc(gs_ready, 1)

            def finish(i):
                dve.wait_ge(down_done, i * E - E)
                dve.wait_ge(kept_ready, i - 1)
                nc.vector.tensor_tensor(o_sb[:, :], ps_y[:, 0:T], x1_kept[:, :], ALU.add).then_inc(out_ready, 1)

            def one_pass(i, with_tail, with_finish):
                for p in range(NPOS):
                    split_lo(i, p)
                    if not with_tail:
                        weights(p)
                    if with_tail:
                        tail(i, p)
                    if with_finish:
                        experts(i - 1, p + NPOS)
                        if p == V_FINISH:
                            finish(i)
                    if with_tail:
                        experts(i, p)
                    user(i, p)

            one_pass(0, False, False)
            one_pass(1, True, False)
            with dve.Fori(2, NB) as i:
                one_pass(i, True, True)
            for p in range(NPOS):
                tail(NB, p)
                experts(NB - 1, p + NPOS)
                if p == V_FINISH:
                    finish(NB)
                experts(NB, p)
            for p in range(NPOS, 2 * NPOS):
                experts(NB, p)
            finish(NB + 1)

        @block.tensor
        def _(pe):
            pe.wait_ge(first_landed, N_FIRST)
            pe.wait_ge(bias_ready, len(pick_raw) + 1)

            def h_group(b, slot, at, tiles):
                nc.tensor.matmul(ps_h[b][:, 0:tiles * D], pick_sb[:, 0:P], cw_parts[:, 0:tiles * D],
                                 start=True, stop=False)
                for k in range(tiles):
                    last = nc.tensor.matmul(ps_h[b][:, k * D:(k + 1) * D],
                                            raw[I0 + slot][:, at + k * P:at + (k + 1) * P], w_item_sb[:, :],
                                            start=False, stop=(k == tiles - 1))
                last.then_inc(h_product, 1)

            def h_pair(s, landed, free):
                pe.wait_ge(item_landed[s], landed)
                for half in range(2):
                    if free is not None:
                        pe.wait_ge(h_ready, free + half)
                    h_group((2 * s + half) % 4, s, half * GD, GT)

            h_pair(0, 16, None)
            h_pair(1, 16, None)
            for s in range(2, ISLOTS):
                h_pair(s, 16, 2 * s - 3)
            with pe.Fori(1, NPAIR // ISLOTS) as r:
                for s in range(ISLOTS):
                    h_pair(s, r * 16 + 16, r * (2 * ISLOTS) + (2 * s - 3))
            h_pair(0, 16 * (NPAIR // ISLOTS + 1), NG - 5)
            pe.wait_ge(item_landed[1], 16 * (NPAIR // ISLOTS + 1))
            pe.wait_ge(h_ready, NG - 3)
            h_group(NG % 4, 1, 0, 1)
            pe.wait_ge(h_ready, NG + 1)
            pe.wait_ge(const_landed, N_CONST)

            def adj_step(i, p):
                q = p % SPL
                pe.wait_ge(lo_ready, i * NPOS + (p + 1))
                tiles = CT if p < NC else 1
                rows = P if p < NC else KREM
                for c in range(tiles):
                    k = p * CT + c
                    w_hi = h_hi[0:rows, k * D:(k + 1) * D]
                    w_lo = h_lo[0:rows, k * D:(k + 1) * D]
                    m_hi = a_hi[q][0:rows, c * T:(c + 1) * T]
                    m_lo = a_lo[q][0:rows, c * T:(c + 1) * T]
                    nc.tensor.matmul(acc[:, 0:T], w_hi, m_hi, start=(k == 0), stop=False)
                    nc.tensor.matmul(acc[:, 0:T], w_hi, m_lo, start=False, stop=False)
                    last = nc.tensor.matmul(acc[:, 0:T], w_lo, m_hi, start=False, stop=(k == KT))
                last.then_inc(adj_used, 1)

            def back(rows, done):
                for q in range(Q):
                    last = nc.tensor.transpose(ps_x[:, q * TQ:(q + 1) * TQ], rows[0:TQ, q * D:(q + 1) * D],
                                               ident_sb[0:TQ, 0:TQ])
                last.then_inc(done, 1)

            def user(i, p):
                if p == U_TURN:
                    pe.wait_ge(u_normed, i + 1)
                    back(xr_sb, u_turned)
                if p == U_DENSE:
                    pe.wait_ge(u_kept, i + 1)
                    nc.tensor.matmul(acc[:, 0:T], w_user_sb[:, :], xn_sb[:, :], start=False, stop=False).then_inc(u_dense, 1)

            def down(i, e):
                for j in range(HH):
                    pe.wait_ge(gs_ready, i * (E * HH) + (HH * (e - E) + j + 1))
                    last = nc.tensor.matmul(ps_y[:, 0:T], w2_sb[:, (e * HH + j) * D:(e * HH + j + 1) * D],
                                            gs_sb[e % 2][j][:, :], start=False, stop=(e == E - 1 and j == HH - 1))
                last.then_inc(down_done, 1)

            def tail(i, p):
                if p == T_TURN:
                    pe.wait_ge(x1_ready, i)
                    for q in range(Q):
                        last = nc.tensor.transpose(ps_v[0:TQ, q * D:(q + 1) * D], x1_sb[:, q * TQ:(q + 1) * TQ],
                                                   ident_sb[:, :])
                    last.then_inc(t_turned, 1)
                if p == T_BACK:
                    pe.wait_ge(t_normed, i)
                    back(xt_sb, t_back)
                if p == T_GATE:
                    pe.wait_ge(xn_ready, i)
                    for q in range(Q):
                        last = nc.tensor.matmul(ps_g[0:TQ, q * E:(q + 1) * E], xn_sb[:, q * TQ:(q + 1) * TQ],
                                                gate_w_sb[:, :], start=True, stop=True)
                    last.then_inc(logits_done, 1)
                if p == T_TRANS:
                    pe.wait_ge(cw_ready, i)
                    for q in range(Q):
                        last = nc.tensor.transpose(ps_g[0:E, q * TQ:(q + 1) * TQ], cw_sb[:, q * E:(q + 1) * E],
                                                   ident_sb[0:TQ, 0:TQ])
                    last.then_inc(cwT_done, 1)

            def experts(i, p):
                if p in STARTS[:E]:
                    e = STARTS.index(p)
                    if e == 0:
                        pe.wait_ge(xn_hi_ready, i)
                        pe.wait_ge(xn_lo_ready, i)
                    else:
                        pe.wait_ge(gelu_ready, i * (E * HH) + HH * (e - E))
                    for j in range(HH):
                        at = e * H + j * P
                        nc.tensor.matmul(ps_z[j][:, 0:T], w1_hi[:, at:at + P], xn_hi[:, :], start=True, stop=False)
                        nc.tensor.matmul(ps_z[j][:, 0:T], w1_hi[:, at:at + P], xn_lo[:, :], start=False, stop=False)
                        nc.tensor.matmul(ps_z[j][:, 0:T], w1_lo[:, at:at + P], xn_hi[:, :], start=False,
                                         stop=True).then_inc(z_done, 1)
                    if e == 1:
                        if not (isinstance(i, int) and i == 1):
                            pe.wait_ge(out_ready, i - 1)
                        nc.tensor.matmul(ps_y[:, 0:T], b2_hi[:, :], cw_parts[:, :], start=True, stop=False)
                        nc.tensor.matmul(ps_y[:, 0:T], b2_lo[:, :], cw_parts[:, :], start=False, stop=False)
                    if e > 0:
                        down(i, e - 1)
                    else:
                        pe.wait_ge(parts_ready, i)
                    nc.tensor.matmul(ps_w[:, 0:T], pick_sb[:, e * P:(e + 1) * P], cw_parts[:, :], start=True,
                                     stop=True).then_inc(spread_done, 1)
                if p == STARTS[E]:
                    down(i, E - 1)

            def one_pass(i, with_tail, with_finish):
                for p in range(NPOS):
                    if p == 0 and with_tail:
                        pe.wait_ge(relu_ready, i)
                    adj_step(i, p)
                    if with_tail:
                        tail(i, p)
                    if with_finish:
                        experts(i - 1, p + NPOS)
                    if with_tail:
                        experts(i, p)
                    user(i, p)

            one_pass(0, False, False)
            pe.wait_ge(w_ready, len(w1_raw) + 2)
            one_pass(1, True, False)
            with pe.Fori(2, NB) as i:
                one_pass(i, True, True)
            for p in range(NPOS):
                tail(NB, p)
                experts(NB - 1, p + NPOS)
                experts(NB, p)
            for p in range(NPOS, 2 * NPOS):
                experts(NB, p)


def kernel(x, adj, L0_gnn_item_feat, L0_gnn_W_item, L0_gnn_b_item, L0_gnn_W_user, L0_gnn_b_user, L0_ffn_gate_w,
           L0_ffn_gate_b, L0_ffn_W1, L0_ffn_b1, L0_ffn_W2, L0_ffn_b2):
    import numpy as _np
    import concourse.bacc as _bacc
    from concourse import mybir as _mybir
    from concourse.bass_utils import run_bass_kernel_spmd as _run

    x, adj, item, w_item, b_item, w_user, b_user, gate_w, gate_b, w1, b1, w2, b2 = (
        _np.asarray(a) for a in (x, adj, L0_gnn_item_feat, L0_gnn_W_item, L0_gnn_b_item, L0_gnn_W_user, L0_gnn_b_user,
                                 L0_ffn_gate_w, L0_ffn_gate_b, L0_ffn_W1, L0_ffn_b1, L0_ffn_W2, L0_ffn_b2))
    eye = _np.eye(P, dtype=_np.float32)
    before = _np.tril(_np.ones((E, E), _np.float32), -1)
    pick = _np.zeros((SEL_K, E, P), _np.float32)
    for e in range(E):
        pick[e, e] = pick[LO_ROW + e, e] = 1.0
    b2_rows = _np.zeros((SEL_K, D), _np.float32)
    b2_rows[0:E] = b2
    b2_rows[LO_ROW:SEL_K] = b2
    blocks = adj.reshape(NB, T, N)
    arrays = {
        "adj_main": blocks[:, :, :KT * P].reshape(NB, T, NC, CT, P).transpose(0, 2, 4, 3, 1).reshape(NB, NC, P, CT * T),
        "adj_rem": blocks[:, :, KT * P:].transpose(0, 2, 1),
        "xT": x.reshape(NB, T, D).transpose(0, 2, 1),
        "xR": x.reshape(NB, Q, TQ, D).transpose(0, 2, 1, 3).reshape(NB, TQ, Q * D),
        "itemT": item[:KT * P].reshape(NPAIR, 2 * GT * P, D).transpose(0, 2, 1),
        "item_rem": item[KT * P:].T,
        "w_itemT": w_item.T,
        "b_item": b_item.reshape(1, D),
        "w_userT": w_user.T,
        "b_user": b_user.reshape(D, 1),
        "gate_w": gate_w,
        "gate_b_rows": _np.broadcast_to(_np.tile(gate_b, Q), (P, Q * E)),
        "w1": w1.transpose(1, 0, 2).reshape(D, E * H),
        "b1": b1.reshape(E * HH, P).T,
        "w2": w2.reshape(E * HH, P, D).transpose(1, 0, 2).reshape(P, E * HH * D),
        "b2": b2_rows,
        "ident": eye,
        "before": _np.broadcast_to(_np.tile(before.reshape(-1), Q), (P, Q * E * E)),
        "pick": pick.reshape(SEL_K, E * P),
    }
    arrays = {f"in_{name}": _np.ascontiguousarray(a) for name, a in arrays.items()}
    nc = _bacc.Bacc("TRN2", target_bir_lowering=False, num_devices=1)
    args = [nc.dram_tensor(name, a.shape, _mybir.dt.from_np(a.dtype), kind="ExternalInput").ap()
            for name, a in arrays.items()]
    args.append(nc.dram_tensor("out", (NB, D, T), _mybir.dt.float32, kind="ExternalOutput").ap())
    build(nc, *args)
    r = _run(nc, [arrays], core_ids=[0])
    return r.results[0]["out"].transpose(0, 2, 1).reshape(N, D)
```

```python
import concourse.bass as bass
from concourse import mybir
from contextlib import ExitStack

import numpy as np

P = 128
N = 10000
D = 128
E = 8
H = 256
HH = H // P
T = 500
NB = N // T
Q = 4
TQ = T // Q
KT = N // P
KREM = N - KT * P
CT = 2
NC = KT // CT
NPOS = NC + 1
RAW = 5
SPL = 4
GT = 3
GD = GT * D
NG = KT // GT
NPAIR = NG // 2
ISLOTS = 4
I0 = RAW - ISLOTS
EPS = 1e-5
LO_ROW = 32
SEL_K = LO_ROW + E
GS = 9

assert NC * CT == KT and NG * GT == KT and NPAIR * 2 == NG and NPAIR % ISLOTS == 1
assert NPOS % RAW == 0 and NPOS % SPL == 0

T_TURN, T_BACK, T_GATE, T_TRANS = 2, 10, 13, 23
U_TURN, U_DENSE = 35, 38
STARTS = (27, 31, 35, 39, 44, 49, 54, 59)
NSPLIT = 6
DOWN = [8 if e < NSPLIT else 6 for e in range(E)]
W_SPLIT = 16
A_RELU, A_TOKEN, A_NORM, A_EXP, A_SPLIT, A_SPREAD, A_STORE, A_KEEP, A_USER, A_FFN, A_SCALED = 2, 5, 12, 17, 25, 26, 31, 37, 38, 4, 6
V_X1, V_STATS, V_NORM, V_LO, V_FINISH, V_USTATS, V_UNORM, V_FFN, V_SCALED = 2, 7, 9, 25, 29, 12, 34, 4, 7
V_LOGITS, V_PROB, V_COMPARE, V_RANK, V_WEIGHT, V_SPREAD = 16, 18, 20, 21, 22, 26


def build(nc, adj_main, adj_rem, xT, xR, itemT, item_rem, w_itemT, b_item, w_userT, b_user, gate_w,
          gate_b_rows, w1, b1, w2, b2, ident, before, pick, outT):
    fp32 = mybir.dt.float32
    fp32r = mybir.dt.float32r
    ALU = mybir.AluOpType
    ACT = mybir.ActivationFunctionType
    AX = mybir.AxisListType

    with ExitStack() as ctx:
        def sb(name, shape, dt=fp32):
            return ctx.enter_context(nc.sbuf_tensor(name, shape, dt))

        def bank(name):
            return ctx.enter_context(nc.psum_tensor(name, [P, 512], fp32))

        def sem(name):
            return ctx.enter_context(nc.semaphore(name))

        h_hi = sb("h_hi", [P, (KT + 1) * D], fp32r)
        h_lo = sb("h_lo", [P, (KT + 1) * D], fp32r)
        raw = [sb(f"raw{s}", [P, CT * T]) for s in range(RAW)]
        a_hi = [sb(f"a_hi{s}", [P, CT * T], fp32r) for s in range(SPL)]
        a_lo = [sb(f"a_lo{s}", [P, CT * T], fp32r) for s in range(SPL)]
        w_item_sb = sb("w_item_sb", [P, D])
        w_user_sb = sb("w_user_sb", [P, D])
        b_user_sb = sb("b_user_sb", [P, 1])
        gate_w_sb = sb("gate_w_sb", [P, E])
        gate_b_sb = sb("gate_b_sb", [P, Q * E])
        w1_hi = sb("w1_hi", [P, E * H], fp32r)
        w1_lo = sb("w1_lo", [P, E * H], fp32r)
        b1_sb = sb("b1_sb", [P, E * HH])
        w2_hi = sb("w2_hi", [P, NSPLIT * HH * D], fp32r)
        w2_lo = sb("w2_lo", [P, NSPLIT * HH * D], fp32r)
        w2_sb = sb("w2_sb", [P, (E - NSPLIT) * HH * D])
        b2_hi = sb("b2_hi", [SEL_K, D], fp32r)
        b2_lo = sb("b2_lo", [SEL_K, D], fp32r)
        ident_sb = sb("ident_sb", [P, P])
        before_sb = sb("before_sb", [P, E * E])
        pick_sb = sb("pick_sb", [SEL_K, E * P], fp32r)
        power_sb = sb("power_sb", [TQ, Q])
        x_sb = sb("x_sb", [P, T])
        r_sb = sb("r_sb", [P, T])
        x1_sb = sb("x1_sb", [P, T])
        x1_kept = sb("x1_kept", [P, T])
        xn_sb = sb("xn_sb", [P, T])
        xn_hi = sb("xn_hi", [P, T], fp32r)
        xn_lo = sb("xn_lo", [P, T], fp32r)
        xr_sb = sb("xr_sb", [P, Q * D])
        xt_sb = sb("xt_sb", [P, Q * D])
        stats_sb = [sb(f"stats_sb{n}", [TQ, Q * 6]) for n in range(2)]
        mv_sb = [sb(f"mv_sb{n}", [TQ, Q * 2]) for n in range(2)]
        var_sb = [sb(f"var_sb{n}", [TQ, Q]) for n in range(2)]
        rstd_sb = [sb(f"rstd_sb{n}", [TQ, Q]) for n in range(2)]
        logit_sb = sb("logit_sb", [TQ, Q * E])
        top_sb = sb("top_sb", [TQ, Q])
        shift_sb = sb("shift_sb", [TQ, Q * E])
        exp_sb = sb("exp_sb", [TQ, Q * E])
        sum_sb = sb("sum_sb", [TQ, Q])
        inv_sb = sb("inv_sb", [TQ, Q])
        prob_sb = sb("prob_sb", [TQ, Q * E])
        rank_sb = sb("rank_sb", [TQ, Q * E])
        cw_sb = sb("cw_sb", [TQ, Q * E])
        cw_parts = sb("cw_parts", [SEL_K, T], fp32r)
        g_sb = [sb(f"g_sb{j}", [P, T]) for j in range(HH)]
        gs_hi = [[sb(f"gs_hi{s}_{j}", [P, T], fp32r) for j in range(HH)] for s in range(2)]
        gs_sb = [sb(f"gs_sb{j}", [P, T]) for j in range(HH)]
        gs_lo = [sb(f"gs_lo{j}", [P, T], fp32r) for j in range(HH)]
        o_sb = r_sb
        gt_sb = xt_sb[0:TQ, 0:Q * E * E]
        eq_sb = xt_sb[0:TQ, Q * E * E:2 * Q * E * E]

        acc = bank("acc")
        ps_x = bank("ps_x")
        ps_v = bank("ps_v")
        ps_g = bank("ps_g")
        ps_w = bank("ps_w")
        ps_z = [bank(f"ps_z{j}") for j in range(HH)]
        ps_y = bank("ps_y")
        ps_h = [ps_x, ps_v, ps_g, ps_w]

        w_item_landed = sem("w_item_landed")
        b_item_landed = sem("b_item_landed")
        pick_landed = [sem(f"pick_landed{n}") for n in range(2)]
        const_landed = sem("const_landed")
        item_landed = [sem(f"item_landed{s}") for s in range(ISLOTS)]
        bias_hi_ready = sem("bias_hi_ready")
        bias_ready = sem("bias_ready")
        h_product = sem("h_product")
        h_hi_ready = sem("h_hi_ready")
        h_ready = sem("h_ready")
        w_hi_ready = sem("w_hi_ready")
        w_ready = sem("w_ready")
        w2_landed = [sem(f"w2_landed{n}") for n in range(-(-NSPLIT * HH * D // T))]
        power_ready = sem("power_ready")
        raw_landed = [sem(f"raw_landed{s}") for s in range(RAW)]
        hi_ready = sem("hi_ready")
        lo_ready = sem("lo_ready")
        adj_used = sem("adj_used")
        x_landed = sem("x_landed")
        xr_landed = sem("xr_landed")
        u_stats = sem("u_stats")
        u_moments = sem("u_moments")
        u_var = sem("u_var")
        u_rstd = sem("u_rstd")
        u_normed = sem("u_normed")
        u_turned = sem("u_turned")
        u_kept = sem("u_kept")
        u_dense = sem("u_dense")
        relu_ready = sem("relu_ready")
        x1_ready = sem("x1_ready")
        t_turned = sem("t_turned")
        xt_ready = sem("xt_ready")
        t_stats = sem("t_stats")
        t_moments = sem("t_moments")
        var_clear = sem("var_clear")
        t_var = sem("t_var")
        t_rstd = sem("t_rstd")
        t_normed = sem("t_normed")
        t_back = sem("t_back")
        xn_hi_ready = sem("xn_hi_ready")
        xn_ready = sem("xn_ready")
        xn_lo_ready = sem("xn_lo_ready")
        logits_done = sem("logits_done")
        gate_step = sem("gate_step")
        shift_ready = sem("shift_ready")
        exp_ready = sem("exp_ready")
        rank_ready = sem("rank_ready")
        cw_ready = sem("cw_ready")
        cwT_done = sem("cwT_done")
        cw_hi_ready = sem("cw_hi_ready")
        parts_ready = sem("parts_ready")
        z_done = sem("z_done")
        spread_done = sem("spread_done")
        gelu_ready = sem("gelu_ready")
        gs_ready = sem("gs_ready")
        gs_hi_ready = sem("gs_hi_ready")
        gs_lo_ready = sem("gs_lo_ready")
        down_done = sem("down_done")
        kept_ready = sem("kept_ready")
        out_ready = sem("out_ready")
        stored = sem("stored")

        block = ctx.enter_context(nc.Block())

        def val(ap):
            return ap.bitcast(fp32)

        def quarters(ap, width):
            return ap.rearrange("p (q c) -> p q c", c=width)

        b_item_raw = xn_sb
        b2_raw = xt_sb
        landing = [g_sb[0], g_sb[1], r_sb, x1_sb, x1_kept]

        def pieces(width):
            return [(landing[n], at, min(T, width - at)) for n, at in enumerate(range(0, width, T))]

        w1_pieces = pieces(E * H)
        w2_pieces = pieces(NSPLIT * HH * D)
        weight_parts = [(hi[:, at:at + width], lo[:, at:at + width], landed[:, 0:width])
                        for hi, lo, parts in ((w1_hi, w1_lo, w1_pieces), (w2_hi, w2_lo, w2_pieces))
                        for landed, at, width in parts]
        half = E * P // 2
        pick_parts = [(slice(n * half, (n + 1) * half), raw[0][n * 64:n * 64 + SEL_K, 0:half]) for n in range(2)]
        consts = [(ident_sb, ident), (w_user_sb, w_userT), (b_user_sb, b_user), (gate_w_sb, gate_w),
                  (gate_b_sb, gate_b_rows), (b1_sb, b1), (w2_sb, w2[:, NSPLIT * HH * D:]),
                  (before_sb, before)]
        N_CONST = 16 * (len(consts) + 1 + len(w1_pieces))

        @block.sync
        def _(sp):
            def load_items(n, s):
                sp.dma_start(raw[I0 + s][:, 0:2 * GD], itemT[n]).then_inc(item_landed[s], 16)

            def load_step(i, p):
                s = p % RAW
                if isinstance(i, int) and i == 0 and p < RAW:
                    if s == 0:
                        sp.wait_ge(bias_ready, 3)
                    if s >= I0:
                        sp.wait_ge(h_product, NG + 1)
                else:
                    sp.wait_ge(lo_ready, i * NPOS + (p - RAW + 1))
                if p < NC:
                    sp.dma_start(raw[s][:, :], adj_main[i, p]).then_inc(raw_landed[s], 16)
                else:
                    sp.dma_start(raw[s][0:KREM, 0:T], adj_rem[i]).then_inc(raw_landed[s], 16)

            def load_xr(i):
                sp.dma_start(xr_sb[0:TQ, :], xR[i]).then_inc(xr_landed, 16)

            def load_x(i):
                sp.dma_start(x_sb[:, :], xT[i]).then_inc(x_landed, 16)

            for s in range(ISLOTS):
                load_items(s, s)
            with sp.Fori(1, NPAIR // ISLOTS) as r:
                for s in range(ISLOTS):
                    sp.wait_ge(h_product, r * (2 * ISLOTS) + (2 * s + 2 - 2 * ISLOTS))
                    load_items(r * ISLOTS + s, s)
            sp.wait_ge(h_product, NG - 2 * ISLOTS)
            load_items(NPAIR - 1, 0)
            sp.wait_ge(h_product, NG - 2 * ISLOTS + 2)
            sp.dma_start(raw[I0 + 1][:, 0:KREM], item_rem).then_inc(item_landed[1], 16)

            for p in range(NPOS):
                load_step(0, p)
                if p == I0 - 1:
                    load_xr(0)
                if p == RAW:
                    load_x(0)
            with sp.Fori(1, NB) as i:
                for p in range(NPOS):
                    load_step(i, p)
                    if p == 2:
                        sp.wait_ge(u_turned, i)
                        load_xr(i)
                    if p == RAW:
                        sp.wait_ge(x1_ready, i)
                        load_x(i)

        @block.gpsimd
        def _(pool):
            nc.gpsimd.memset(power_sb[:, :], -0.5).then_inc(power_ready, 1)
            for dst, src in consts:
                pool.dma_start(dst[:, :], src).then_inc(const_landed, 16)
            pool.dma_start(b2_raw[0:SEL_K, 0:D], b2).then_inc(const_landed, 16)
            for landed, at, width in w1_pieces:
                pool.dma_start(landed[:, 0:width], w1[:, at:at + width]).then_inc(const_landed, 16)
            pool.wait_ge(power_ready, 1)

            def user(i):
                pool.wait_ge(u_var, i + 1)
                nc.gpsimd.tensor_tensor(rstd_sb[0][:, :], var_sb[0][:, :], power_sb[:, :], ALU.pow).then_inc(u_rstd, 1)

            def tail(i):
                pool.wait_ge(t_var, i)
                nc.gpsimd.tensor_tensor(rstd_sb[1][:, :], var_sb[1][:, :], power_sb[:, :], ALU.pow).then_inc(t_rstd, 1)

            user(0)
            for n, (landed, at, width) in enumerate(w2_pieces):
                pool.wait_ge(w_ready, 2 + n + 1)
                pool.dma_start(landed[:, 0:width], w2[:, at:at + width]).then_inc(w2_landed[n], 16)
            with pool.Fori(1, NB) as i:
                tail(i)
                user(i)
            tail(NB)

        @block.scalar
        def _(act):
            act.dma_start(b_item_raw[0:1, 0:D], b_item).then_inc(b_item_landed, 16)
            act.dma_start(w_item_sb[:, :], w_itemT).then_inc(w_item_landed, 16)
            for n, (cols, landed) in enumerate(pick_parts):
                act.dma_start(landed, pick[:, cols]).then_inc(pick_landed[n], 16)

            def h_hi_part(b, at, rows, cols, product):
                act.wait_ge(h_product, product)
                nc.scalar.activation(h_hi[0:rows, at], ps_h[b][0:rows, 0:cols], ACT.Copy).then_inc(h_hi_ready, 1)

            with act.Fori(0, NG // 4) as r:
                for b in range(4):
                    h_hi_part(b, bass.ds(r * (4 * GD) + b * GD, GD), P, GD, r * 4 + (b + 1))
            for b in range(NG % 4):
                g = NG // 4 * 4 + b
                h_hi_part(b, slice(g * GD, (g + 1) * GD), P, GD, g + 1)
            h_hi_part(NG % 4, slice(KT * D, (KT + 1) * D), KREM, D, NG + 1)

            def split_hi(i, p):
                s, q = p % RAW, p % SPL
                act.wait_ge(raw_landed[s], i * (16 * (NPOS // RAW)) + 16 * (p // RAW + 1))
                if not (isinstance(i, int) and i == 0 and p < SPL):
                    act.wait_ge(adj_used, i * NPOS + (p - SPL + 1))
                rows, cols = (P, CT * T) if p < NC else (KREM, T)
                nc.scalar.activation(a_hi[q][0:rows, 0:cols], raw[s][0:rows, 0:cols],
                                     ACT.Copy).then_inc(hi_ready, 1)

            def weights(p):
                n, odd = divmod(p - W_SPLIT, 2)
                if p >= W_SPLIT and odd == 0 and n < len(weight_parts):
                    hi, _, landed = weight_parts[n]
                    if n < len(w1_pieces):
                        act.wait_ge(const_landed, N_CONST)
                    else:
                        act.wait_ge(w2_landed[n - len(w1_pieces)], 16)
                    nc.scalar.activation(hi, landed, ACT.Copy).then_inc(w_hi_ready, 1)

            def user(i, p):
                if p == A_USER:
                    act.wait_ge(u_turned, i + 1)
                    nc.scalar.activation(xn_sb[:, :], ps_x[:, 0:T], ACT.Copy).then_inc(u_kept, 1)

            def tail(i, p):
                if p == A_RELU:
                    act.wait_ge(adj_used, i * NPOS)
                    nc.scalar.activation(r_sb[:, :], acc[:, 0:T], ACT.Relu, bias=b_user_sb[:, 0:1]).then_inc(relu_ready, 1)
                if p == A_TOKEN:
                    act.wait_ge(t_turned, i)
                    nc.scalar.activation(xt_sb[0:TQ, :], ps_v[0:TQ, :], ACT.Copy).then_inc(xt_ready, 1)
                if p == A_NORM:
                    act.wait_ge(t_back, i)
                    nc.scalar.activation(xn_sb[:, :], ps_x[:, 0:T], ACT.Copy).then_inc(xn_ready, 1)
                if p == A_SPLIT:
                    act.wait_ge(xn_ready, i)
                    if not (isinstance(i, int) and i == 1):
                        act.wait_ge(z_done, i * (E * HH) - E * HH)
                    nc.scalar.activation(xn_hi[:, :], xn_sb[:, :], ACT.Copy).then_inc(xn_hi_ready, 1)
                if p == A_EXP:
                    act.wait_ge(shift_ready, i)
                    nc.scalar.activation(exp_sb[:, :], shift_sb[:, :], ACT.Exp).then_inc(exp_ready, 1)
                if p == A_KEEP:
                    if not (isinstance(i, int) and i == 1):
                        act.wait_ge(out_ready, i - 1)
                        act.wait_ge(stored, i * 16 - 16)
                    act.wait_ge(x1_ready, i)
                    nc.scalar.activation(x1_kept[:, :], x1_sb[:, :], ACT.Copy).then_inc(kept_ready, 1)
                if p == A_SPREAD:
                    act.wait_ge(cwT_done, i)
                    nc.scalar.activation(cw_parts[0:E, :], ps_g[0:E, 0:T], ACT.Copy).then_inc(cw_hi_ready, 1)

            def experts(i, p):
                if p - A_FFN in STARTS:
                    e = STARTS.index(p - A_FFN)
                    if not (isinstance(i, int) and i == 1 and e == 0):
                        if 0 < e <= NSPLIT:
                            act.wait_ge(gs_lo_ready, i * (NSPLIT * HH) + HH * (e - NSPLIT))
                        else:
                            act.wait_ge(gs_ready, i * (E * HH) + HH * (e - E))
                    for j in range(HH):
                        act.wait_ge(z_done, i * (E * HH) + (HH * (e - E) + j + 1))
                        nc.scalar.activation(g_sb[j][:, :], ps_z[j][:, 0:T], ACT.Gelu,
                                             bias=b1_sb[:, e * HH + j:e * HH + j + 1]).then_inc(gelu_ready, 1)
                if p - A_SCALED in STARTS[:NSPLIT]:
                    e = STARTS.index(p - A_SCALED)
                    if not (isinstance(i, int) and i == 1 and e < 2):
                        act.wait_ge(down_done, i * E + (e - E - 1))
                    for j in range(HH):
                        act.wait_ge(gs_ready, i * (E * HH) + (HH * (e - E) + j + 1))
                        nc.scalar.activation(gs_hi[e % 2][j][:, :], g_sb[j][:, :], ACT.Copy).then_inc(gs_hi_ready, 1)

            def finish(i):
                act.wait_ge(out_ready, i - 1)
                act.dma_start(outT[i - 2], o_sb[:, :]).then_inc(stored, 16)

            def one_pass(i, with_tail, with_finish):
                for p in range(NPOS):
                    split_hi(i, p)
                    if not with_tail:
                        weights(p)
                    if with_tail:
                        tail(i, p)
                    if with_finish:
                        experts(i - 1, p + NPOS)
                        if p == A_STORE:
                            finish(i)
                    if with_tail:
                        experts(i, p)
                    user(i, p)

            one_pass(0, False, False)
            act.wait_ge(w_ready, len(weight_parts) + 2)
            one_pass(1, True, False)
            with act.Fori(2, NB) as i:
                one_pass(i, True, True)
            for p in range(NPOS):
                tail(NB, p)
                experts(NB - 1, p + NPOS)
                if p == A_STORE:
                    finish(NB)
                experts(NB, p)
            for p in range(NPOS, 2 * NPOS):
                experts(NB, p)
            finish(NB + 1)
            act.wait_ge(stored, 16 * NB)

        @block.vector
        def _(dve):
            nc.vector.memset(val(cw_parts[:, :]), 0.0).then_inc(bias_hi_ready, 1)
            dve.wait_ge(b_item_landed, 16)
            dve.wait_ge(bias_hi_ready, 1)
            bias = b_item_raw[0:1, 0:D].unsqueeze(1).to_broadcast([1, GT, D])
            row_hi = quarters(cw_parts[0:1, 0:GD], D)
            nc.vector.tensor_copy(row_hi, bias).then_inc(bias_hi_ready, 1)
            dve.wait_ge(bias_hi_ready, 2)
            nc.vector.tensor_tensor(quarters(cw_parts[LO_ROW:LO_ROW + 1, 0:GD], D), bias, val(row_hi),
                                    ALU.subtract).then_inc(bias_ready, 1)
            for n, (cols, landed) in enumerate(pick_parts):
                dve.wait_ge(pick_landed[n], 16)
                nc.vector.tensor_copy(pick_sb[:, cols], landed).then_inc(bias_ready, 1)

            def h_lo_part(b, at, rows, cols, ready):
                dve.wait_ge(h_hi_ready, ready)
                nc.vector.tensor_tensor(h_lo[0:rows, at], ps_h[b][0:rows, 0:cols], val(h_hi[0:rows, at]),
                                        ALU.subtract).then_inc(h_ready, 1)

            with dve.Fori(0, NG // 4) as r:
                for b in range(4):
                    h_lo_part(b, bass.ds(r * (4 * GD) + b * GD, GD), P, GD, r * 4 + (b + 1))
            for b in range(NG % 4):
                g = NG // 4 * 4 + b
                h_lo_part(b, slice(g * GD, (g + 1) * GD), P, GD, g + 1)
            h_lo_part(NG % 4, slice(KT * D, (KT + 1) * D), KREM, D, NG + 1)

            def split_lo(i, p):
                s, q = p % RAW, p % SPL
                dve.wait_ge(hi_ready, i * NPOS + (p + 1))
                rows, cols = (P, CT * T) if p < NC else (KREM, T)
                nc.vector.tensor_tensor(a_lo[q][0:rows, 0:cols], raw[s][0:rows, 0:cols],
                                        val(a_hi[q][0:rows, 0:cols]), ALU.subtract).then_inc(lo_ready, 1)

            def weights(p):
                n, odd = divmod(p - W_SPLIT, 2)
                if p >= W_SPLIT and odd == 1 and n < len(weight_parts):
                    hi, lo, landed = weight_parts[n]
                    dve.wait_ge(w_hi_ready, n + 1)
                    nc.vector.tensor_tensor(lo, landed, val(hi), ALU.subtract).then_inc(w_ready, 1)
                if p == W_SPLIT:
                    dve.wait_ge(const_landed, N_CONST)
                    nc.vector.tensor_copy(b2_hi[:, :], b2_raw[0:SEL_K, 0:D]).then_inc(w_ready, 1)
                    dve.wait_ge(w_ready, 1)
                    nc.vector.tensor_tensor(b2_lo[:, :], b2_raw[0:SEL_K, 0:D], val(b2_hi[:, :]),
                                            ALU.subtract).then_inc(w_ready, 1)

            def moments(n, rows, stats_done, moments_done, var_done, count):
                for q in range(Q):
                    last = nc.vector.bn_stats(stats_sb[n][:, q * 6:(q + 1) * 6], rows[:, q * D:(q + 1) * D])
                last.then_inc(stats_done, 1)
                dve.wait_ge(stats_done, count)
                nc.vector.memset(var_sb[n][:, :], 0.0).then_inc(var_clear, 1)
                for q in range(Q):
                    last = nc.vector.bn_aggr(mv_sb[n][:, q * 2:(q + 1) * 2], stats_sb[n][:, q * 6:(q + 1) * 6])
                last.then_inc(moments_done, 1)
                dve.wait_ge(moments_done, count)
                nc.vector.tensor_scalar(var_sb[n][:, :], quarters(mv_sb[n][:, :], 2)[:, :, 1], EPS, None,
                                        ALU.add).then_inc(var_done, 1)

            def normalise(n, out, rows, done):
                for q in range(Q):
                    last = nc.vector.tensor_scalar(out[:, q * D:(q + 1) * D], rows[:, q * D:(q + 1) * D],
                                                   mv_sb[n][:, 2 * q:2 * q + 1], rstd_sb[n][:, q:q + 1],
                                                   ALU.subtract, ALU.mult)
                last.then_inc(done, 1)

            def user(i, p):
                if p == V_USTATS:
                    dve.wait_ge(xr_landed, i * 16 + 16)
                    moments(0, xr_sb[0:TQ, :], u_stats, u_moments, u_var, i + 1)
                if p == V_UNORM:
                    dve.wait_ge(u_rstd, i + 1)
                    normalise(0, xr_sb[0:TQ, :], xr_sb[0:TQ, :], u_normed)

            def tail(i, p):
                if p == V_X1:
                    dve.wait_ge(relu_ready, i)
                    dve.wait_ge(x_landed, i * 16)
                    if not (isinstance(i, int) and i == 1):
                        dve.wait_ge(kept_ready, i - 1)
                    nc.vector.tensor_tensor(x1_sb[:, :], x_sb[:, :], r_sb[:, :], ALU.add).then_inc(x1_ready, 1)
                if p == V_STATS:
                    dve.wait_ge(xt_ready, i)
                    moments(1, xt_sb[0:TQ, :], t_stats, t_moments, t_var, i)
                if p == V_NORM:
                    dve.wait_ge(t_rstd, i)
                    normalise(1, xt_sb[0:TQ, :], xt_sb[0:TQ, :], t_normed)
                if p == V_LO:
                    dve.wait_ge(xn_hi_ready, i)
                    nc.vector.tensor_tensor(xn_lo[:, :], xn_sb[:, :], val(xn_hi[:, :]), ALU.subtract).then_inc(xn_lo_ready, 1)
                step = i * GS - GS
                by_e = quarters(logit_sb[:, :], E)
                exp_by_e = quarters(exp_sb[:, :], E)
                prob = quarters(prob_sb[:, :], E)
                if p == V_LOGITS:
                    dve.wait_ge(logits_done, i)
                    nc.vector.tensor_tensor(logit_sb[:, :], ps_g[0:TQ, 0:Q * E], gate_b_sb[0:TQ, :], ALU.add).then_inc(gate_step, 1)
                    dve.wait_ge(gate_step, step + 1)
                    nc.vector.tensor_reduce(top_sb[:, :], by_e, AX.X, ALU.max).then_inc(gate_step, 1)
                    dve.wait_ge(gate_step, step + 2)
                    nc.vector.tensor_tensor(quarters(shift_sb[:, :], E), by_e, top_sb[:, :].unsqueeze(2).to_broadcast([TQ, Q, E]),
                                            ALU.subtract).then_inc(shift_ready, 1)
                if p == V_PROB:
                    dve.wait_ge(exp_ready, i)
                    nc.vector.tensor_reduce(sum_sb[:, :], exp_by_e, AX.X, ALU.add).then_inc(gate_step, 1)
                    dve.wait_ge(gate_step, step + 3)
                    nc.vector.reciprocal(inv_sb[:, :], sum_sb[:, :]).then_inc(gate_step, 1)
                    dve.wait_ge(gate_step, step + 4)
                    nc.vector.tensor_tensor(prob, exp_by_e, inv_sb[:, :].unsqueeze(2).to_broadcast([TQ, Q, E]),
                                            ALU.mult).then_inc(gate_step, 1)
                if p == V_COMPARE:
                    shape = [TQ, Q, E, E]
                    of_e = prob.unsqueeze(3).to_broadcast(shape)
                    of_f = prob.unsqueeze(2).to_broadcast(shape)
                    dve.wait_ge(gate_step, step + 5)
                    nc.vector.tensor_tensor(gt_sb.rearrange("p (q e f) -> p q e f", e=E, f=E), of_f, of_e,
                                            ALU.is_gt).then_inc(gate_step, 1)
                    nc.vector.tensor_tensor(eq_sb.rearrange("p (q e f) -> p q e f", e=E, f=E), of_f, of_e,
                                            ALU.is_equal).then_inc(gate_step, 1)
                if p == V_RANK:
                    dve.wait_ge(gate_step, step + 7)
                    nc.vector.tensor_tensor(quarters(eq_sb, E * E), quarters(eq_sb, E * E),
                                            before_sb[0:TQ, :].unsqueeze(1).to_broadcast([TQ, Q, E * E]),
                                            ALU.mult).then_inc(gate_step, 1)
                    dve.wait_ge(gate_step, step + 8)
                    nc.vector.tensor_tensor(gt_sb, gt_sb, eq_sb, ALU.add).then_inc(gate_step, 1)
                if p == V_WEIGHT:
                    dve.wait_ge(gate_step, step + 9)
                    nc.vector.tensor_reduce(rank_sb[:, :], gt_sb.rearrange("p (c f) -> p c f", f=E),
                                            AX.X, ALU.add).then_inc(rank_ready, 1)
                    dve.wait_ge(rank_ready, i)
                    nc.vector.scalar_tensor_tensor(out=cw_sb[:, :], in0=rank_sb[:, :], scalar=1.5, in1=prob_sb[:, :],
                                                   op0=ALU.is_lt, op1=ALU.mult).then_inc(cw_ready, 1)
                if p == V_SPREAD:
                    dve.wait_ge(cw_hi_ready, i)
                    nc.vector.tensor_tensor(cw_parts[LO_ROW:LO_ROW + E, :], ps_g[0:E, 0:T], val(cw_parts[0:E, :]),
                                            ALU.subtract).then_inc(parts_ready, 1)

            def experts(i, p):
                if p - V_FFN in STARTS:
                    e = STARTS.index(p - V_FFN)
                    dve.wait_ge(spread_done, i * E + (e + 1 - E))
                    if e > NSPLIT:
                        dve.wait_ge(down_done, i * E + (e - E))
                    for j in range(HH):
                        dve.wait_ge(gelu_ready, i * (E * HH) + (HH * (e - E) + j + 1))
                        scaled = g_sb[j] if e < NSPLIT else gs_sb[j]
                        nc.vector.tensor_tensor(scaled[:, :], ps_w[:, 0:T], g_sb[j][:, :],
                                                ALU.mult).then_inc(gs_ready, 1)
                if p - V_SCALED in STARTS[:NSPLIT]:
                    e = STARTS.index(p - V_SCALED)
                    if not (isinstance(i, int) and i == 1 and e == 0):
                        dve.wait_ge(down_done, i * E + (e - E))
                    for j in range(HH):
                        dve.wait_ge(gs_hi_ready, i * (NSPLIT * HH) + (HH * (e - NSPLIT) + j + 1))
                        nc.vector.tensor_tensor(gs_lo[j][:, :], g_sb[j][:, :], val(gs_hi[e % 2][j][:, :]),
                                                ALU.subtract).then_inc(gs_lo_ready, 1)

            def finish(i):
                dve.wait_ge(down_done, i * E - E)
                dve.wait_ge(kept_ready, i - 1)
                nc.vector.tensor_tensor(o_sb[:, :], ps_y[:, 0:T], x1_kept[:, :], ALU.add).then_inc(out_ready, 1)

            def one_pass(i, with_tail, with_finish):
                for p in range(NPOS):
                    split_lo(i, p)
                    if not with_tail:
                        weights(p)
                    if with_tail:
                        tail(i, p)
                    if with_finish:
                        experts(i - 1, p + NPOS)
                        if p == V_FINISH:
                            finish(i)
                    if with_tail:
                        experts(i, p)
                    user(i, p)

            one_pass(0, False, False)
            one_pass(1, True, False)
            with dve.Fori(2, NB) as i:
                one_pass(i, True, True)
            for p in range(NPOS):
                tail(NB, p)
                experts(NB - 1, p + NPOS)
                if p == V_FINISH:
                    finish(NB)
                experts(NB, p)
            for p in range(NPOS, 2 * NPOS):
                experts(NB, p)
            finish(NB + 1)

        @block.tensor
        def _(pe):
            pe.wait_ge(w_item_landed, 16)

            def h_group(b, slot, at, tiles, first=False):
                for k in range(tiles):
                    nc.tensor.matmul(ps_h[b][:, k * D:(k + 1) * D], raw[I0 + slot][:, at + k * P:at + (k + 1) * P],
                                     w_item_sb[:, :], start=(k == 0), stop=False)
                if first:
                    pe.wait_ge(bias_ready, 2)
                nc.tensor.matmul(ps_h[b][:, 0:tiles * D], pick_sb[:, 0:P], cw_parts[:, 0:tiles * D],
                                 start=False, stop=True).then_inc(h_product, 1)

            def h_pair(s, landed, free):
                pe.wait_ge(item_landed[s], landed)
                for half in range(2):
                    if free is not None:
                        pe.wait_ge(h_ready, free + half)
                    h_group((2 * s + half) % 4, s, half * GD, GT, free is None and s == 0 and half == 0)

            h_pair(0, 16, None)
            h_pair(1, 16, None)
            for s in range(2, ISLOTS):
                h_pair(s, 16, 2 * s - 3)
            with pe.Fori(1, NPAIR // ISLOTS) as r:
                for s in range(ISLOTS):
                    h_pair(s, r * 16 + 16, r * (2 * ISLOTS) + (2 * s - 3))
            h_pair(0, 16 * (NPAIR // ISLOTS + 1), NG - 5)
            pe.wait_ge(item_landed[1], 16 * (NPAIR // ISLOTS + 1))
            pe.wait_ge(h_ready, NG - 3)
            h_group(NG % 4, 1, 0, 1)
            pe.wait_ge(h_ready, NG + 1)
            pe.wait_ge(const_landed, N_CONST)

            def adj_step(i, p):
                q = p % SPL
                pe.wait_ge(lo_ready, i * NPOS + (p + 1))
                tiles = CT if p < NC else 1
                rows = P if p < NC else KREM
                for c in range(tiles):
                    k = p * CT + c
                    w_hi = h_hi[0:rows, k * D:(k + 1) * D]
                    w_lo = h_lo[0:rows, k * D:(k + 1) * D]
                    m_hi = a_hi[q][0:rows, c * T:(c + 1) * T]
                    m_lo = a_lo[q][0:rows, c * T:(c + 1) * T]
                    nc.tensor.matmul(acc[:, 0:T], w_hi, m_hi, start=(k == 0), stop=False)
                    nc.tensor.matmul(acc[:, 0:T], w_hi, m_lo, start=False, stop=False)
                    last = nc.tensor.matmul(acc[:, 0:T], w_lo, m_hi, start=False, stop=(k == KT))
                last.then_inc(adj_used, 1)

            def back(rows, done):
                for q in range(Q):
                    last = nc.tensor.transpose(ps_x[:, q * TQ:(q + 1) * TQ], rows[0:TQ, q * D:(q + 1) * D],
                                               ident_sb[0:TQ, 0:TQ])
                last.then_inc(done, 1)

            def user(i, p):
                if p == U_TURN:
                    pe.wait_ge(u_normed, i + 1)
                    back(xr_sb, u_turned)
                if p == U_DENSE:
                    pe.wait_ge(u_kept, i + 1)
                    nc.tensor.matmul(acc[:, 0:T], w_user_sb[:, :], xn_sb[:, :], start=False, stop=False).then_inc(u_dense, 1)

            def down(i, e):
                for j in range(HH):
                    if e < NSPLIT:
                        pe.wait_ge(gs_lo_ready, i * (NSPLIT * HH) + (HH * (e - NSPLIT) + j + 1))
                        cols = slice((e * HH + j) * D, (e * HH + j + 1) * D)
                        nc.tensor.matmul(ps_y[:, 0:T], w2_hi[:, cols], gs_hi[e % 2][j][:, :], start=False, stop=False)
                        nc.tensor.matmul(ps_y[:, 0:T], w2_hi[:, cols], gs_lo[j][:, :], start=False, stop=False)
                        last = nc.tensor.matmul(ps_y[:, 0:T], w2_lo[:, cols], gs_hi[e % 2][j][:, :], start=False, stop=False)
                    else:
                        pe.wait_ge(gs_ready, i * (E * HH) + (HH * (e - E) + j + 1))
                        n = (e - NSPLIT) * HH + j
                        last = nc.tensor.matmul(ps_y[:, 0:T], w2_sb[:, n * D:(n + 1) * D], gs_sb[j][:, :], start=False,
                                         stop=(e == E - 1 and j == HH - 1))
                last.then_inc(down_done, 1)

            def tail(i, p):
                if p == T_TURN:
                    pe.wait_ge(x1_ready, i)
                    for q in range(Q):
                        last = nc.tensor.transpose(ps_v[0:TQ, q * D:(q + 1) * D], x1_sb[:, q * TQ:(q + 1) * TQ],
                                                   ident_sb[:, :])
                    last.then_inc(t_turned, 1)
                if p == T_BACK:
                    pe.wait_ge(t_normed, i)
                    back(xt_sb, t_back)
                if p == T_GATE:
                    pe.wait_ge(xn_ready, i)
                    for q in range(Q):
                        last = nc.tensor.matmul(ps_g[0:TQ, q * E:(q + 1) * E], xn_sb[:, q * TQ:(q + 1) * TQ],
                                                gate_w_sb[:, :], start=True, stop=True)
                    last.then_inc(logits_done, 1)
                if p == T_TRANS:
                    pe.wait_ge(cw_ready, i)
                    for q in range(Q):
                        last = nc.tensor.transpose(ps_g[0:E, q * TQ:(q + 1) * TQ], cw_sb[:, q * E:(q + 1) * E],
                                                   ident_sb[0:TQ, 0:TQ])
                    last.then_inc(cwT_done, 1)

            def experts(i, p):
                if p in STARTS:
                    e = STARTS.index(p)
                    if e == 0:
                        pe.wait_ge(xn_hi_ready, i)
                        pe.wait_ge(xn_lo_ready, i)
                    if not (isinstance(i, int) and i == 1 and e == 0):
                        pe.wait_ge(gelu_ready, i * (E * HH) + HH * (e - E))
                    for j in range(HH):
                        at = e * H + j * P
                        nc.tensor.matmul(ps_z[j][:, 0:T], w1_hi[:, at:at + P], xn_hi[:, :], start=True, stop=False)
                        nc.tensor.matmul(ps_z[j][:, 0:T], w1_hi[:, at:at + P], xn_lo[:, :], start=False, stop=False)
                        nc.tensor.matmul(ps_z[j][:, 0:T], w1_lo[:, at:at + P], xn_hi[:, :], start=False,
                                         stop=True).then_inc(z_done, 1)
                    if e == 0:
                        pe.wait_ge(parts_ready, i)
                    if not (isinstance(i, int) and i == 1 and e == 0):
                        pe.wait_ge(gs_ready, i * (E * HH) + HH * (e - E))
                    nc.tensor.matmul(ps_w[:, 0:T], pick_sb[:, e * P:(e + 1) * P], cw_parts[:, :], start=True,
                                     stop=True).then_inc(spread_done, 1)
                for e in range(E):
                    if p != STARTS[e] + DOWN[e]:
                        continue
                    if e == 0:
                        if not (isinstance(i, int) and i == 1):
                            pe.wait_ge(out_ready, i - 1)
                        nc.tensor.matmul(ps_y[:, 0:T], b2_hi[:, :], cw_parts[:, :], start=True, stop=False)
                        nc.tensor.matmul(ps_y[:, 0:T], b2_lo[:, :], cw_parts[:, :], start=False, stop=False)
                    down(i, e)

            def one_pass(i, with_tail, with_finish):
                for p in range(NPOS):
                    if p == 0 and with_tail:
                        pe.wait_ge(relu_ready, i)
                    adj_step(i, p)
                    if with_tail:
                        tail(i, p)
                    if with_finish:
                        experts(i - 1, p + NPOS)
                    if with_tail:
                        experts(i, p)
                    user(i, p)

            one_pass(0, False, False)
            pe.wait_ge(w_ready, len(weight_parts) + 2)
            one_pass(1, True, False)
            with pe.Fori(2, NB) as i:
                one_pass(i, True, True)
            for p in range(NPOS):
                tail(NB, p)
                experts(NB - 1, p + NPOS)
                experts(NB, p)
            for p in range(NPOS, 2 * NPOS):
                experts(NB, p)


def kernel(x, adj, L0_gnn_item_feat, L0_gnn_W_item, L0_gnn_b_item, L0_gnn_W_user, L0_gnn_b_user, L0_ffn_gate_w,
           L0_ffn_gate_b, L0_ffn_W1, L0_ffn_b1, L0_ffn_W2, L0_ffn_b2):
    import numpy as _np
    import concourse.bacc as _bacc
    from concourse import mybir as _mybir
    from concourse.bass_utils import run_bass_kernel_spmd as _run

    x, adj, item, w_item, b_item, w_user, b_user, gate_w, gate_b, w1, b1, w2, b2 = (
        _np.asarray(a) for a in (x, adj, L0_gnn_item_feat, L0_gnn_W_item, L0_gnn_b_item, L0_gnn_W_user, L0_gnn_b_user,
                                 L0_ffn_gate_w, L0_ffn_gate_b, L0_ffn_W1, L0_ffn_b1, L0_ffn_W2, L0_ffn_b2))
    eye = _np.eye(P, dtype=_np.float32)
    before = _np.tril(_np.ones((E, E), _np.float32), -1)
    pick = _np.zeros((SEL_K, E, P), _np.float32)
    for e in range(E):
        pick[e, e] = pick[LO_ROW + e, e] = 1.0
    b2_rows = _np.zeros((SEL_K, D), _np.float32)
    b2_rows[0:E] = b2
    b2_rows[LO_ROW:SEL_K] = b2
    blocks = adj.reshape(NB, T, N)
    arrays = {
        "adj_main": blocks[:, :, :KT * P].reshape(NB, T, NC, CT, P).transpose(0, 2, 4, 3, 1).reshape(NB, NC, P, CT * T),
        "adj_rem": blocks[:, :, KT * P:].transpose(0, 2, 1),
        "xT": x.reshape(NB, T, D).transpose(0, 2, 1),
        "xR": x.reshape(NB, Q, TQ, D).transpose(0, 2, 1, 3).reshape(NB, TQ, Q * D),
        "itemT": item[:KT * P].reshape(NPAIR, 2 * GT * P, D).transpose(0, 2, 1),
        "item_rem": item[KT * P:].T,
        "w_itemT": w_item.T,
        "b_item": b_item.reshape(1, D),
        "w_userT": w_user.T,
        "b_user": b_user.reshape(D, 1),
        "gate_w": gate_w,
        "gate_b_rows": _np.broadcast_to(_np.tile(gate_b, Q), (P, Q * E)),
        "w1": w1.transpose(1, 0, 2).reshape(D, E * H),
        "b1": b1.reshape(E * HH, P).T,
        "w2": w2.reshape(E * HH, P, D).transpose(1, 0, 2).reshape(P, E * HH * D),
        "b2": b2_rows,
        "ident": eye,
        "before": _np.broadcast_to(before.reshape(-1), (P, E * E)),
        "pick": pick.reshape(SEL_K, E * P),
    }
    arrays = {f"in_{name}": _np.ascontiguousarray(a) for name, a in arrays.items()}
    nc = _bacc.Bacc("TRN2", target_bir_lowering=False, num_devices=1)
    args = [nc.dram_tensor(name, a.shape, _mybir.dt.from_np(a.dtype), kind="ExternalInput").ap()
            for name, a in arrays.items()]
    args.append(nc.dram_tensor("out", (NB, D, T), _mybir.dt.float32, kind="ExternalOutput").ap())
    build(nc, *args)
    r = _run(nc, [arrays], core_ids=[0])
    return r.results[0]["out"].transpose(0, 2, 1).reshape(N, D)
```
